# Optimizing a Trainium2 kernel written in Bass

```python
import numpy as np
import jax
import jax.numpy as jnp

def _softmax(x, axis=-1):
    return jax.nn.softmax(x, axis=axis)

def _gelu(x):
    return jax.nn.gelu(x, approximate=True)

def _silu(x):
    return jax.nn.silu(x)

def _sigmoid(x):
    return jax.nn.sigmoid(x)

def _layernorm(x, axis=-1, eps=1e-05):
    m = jnp.mean(x, axis=axis, keepdims=True)
    v = jnp.var(x, axis=axis, keepdims=True)
    return (x - m) / jnp.sqrt(v + eps)

def _scatter_add(tgt, idx, src, axis=0):
    return tgt.at[idx].add(src)

def _segment_sum(src, seg, n):
    return jax.ops.segment_sum(src, seg, n)
kernel_name = 'mk_decoder_preln_d1_seqx_r8_b842ea'

def setup_inputs(seed: int=0):
    np.random.seed(seed)
    _w = jnp.asarray

    def _rec_inputs():
        import jax
        import jax.numpy as jnp
        _rk = jax.random.key(seed)
        x = -0.0003929 + 0.9999 * jax.random.normal(jax.random.fold_in(_rk, 1), (8, 128, 512), jnp.float32)
        _lenS = 128 - jax.random.randint(jax.random.fold_in(_rk, 7), (8,), 0, max(1, 128 // 4) + 1, jnp.int32)
        _lenS2 = 128 - jax.random.randint(jax.random.fold_in(_rk, 8), (8,), 0, max(1, 128 // 4) + 1, jnp.int32)
        _ctx_4096P = jax.random.normal(jax.random.fold_in(_rk, 11), (8, 16, 512), jnp.float32)
        _ctx_4096c = jax.random.dirichlet(jax.random.fold_in(_rk, 511), 0.3 * jnp.ones((16,), jnp.float32), (8, 128))
        _ctx_4096t = jnp.einsum('bsk,bkd->bsd', _ctx_4096c, _ctx_4096P)
        _ctx_4096t = _ctx_4096t * jax.lax.rsqrt(jnp.mean(jnp.square(_ctx_4096t)) + 1e-12) * 0.953939
        ctx_4096 = 2.81802e-05 + 1.00001 * (_ctx_4096t + 0.3 * jax.random.normal(jax.random.fold_in(_rk, 611), (8, 128, 512), jnp.float32))
        _validS = jnp.arange(128)[None, :] < _lenS[:, None]
        _validS2 = jnp.arange(128)[None, :] < _lenS2[:, None]
        _causal = jnp.tril(jnp.ones((128, 128), dtype=bool))
        mask_BxSxS2_ff0 = jnp.where(jnp.ones((8, 128, 128), dtype=bool), 0.0, -1000000000.0).astype(jnp.float32)
        return (x, ctx_4096, mask_BxSxS2_ff0)
    x, ctx_4096, mask_BxSxS2_ff0 = _rec_inputs()

    def _L0_attn_setup():
        import math
        import jax, jax.numpy as jnp
        import numpy as np
        IN_F, OUT_F, HID = (512, 512, 512)
        WINDOW, STRIPES = (6, 3)

        def make_sparse_mask(n_in=IN_F, n_out=OUT_F, window=WINDOW, stripes=STRIPES):
            m = np.zeros((n_in, n_out), dtype=np.float32)
            stride = int(math.sqrt(n_in))
            for k in range(stripes):
                ps = stride * k
                for i in range(0, n_in, window):
                    m[ps + i:ps + i + window, i:i + window] = 1.0
            mb = m.astype(bool)
            return jnp.asarray((mb | mb.T).astype(np.float32))
        key = jax.random.key(seed)
        k1, k2, k3, k4 = jax.random.split(key, 4)
        scale = 1.0 / math.sqrt(IN_F)
        x = jax.random.normal(k1, (8, 96, IN_F), dtype=jnp.float32)
        w1 = jax.random.normal(k2, (HID, IN_F), dtype=jnp.float32) * scale
        w2 = jax.random.normal(k3, (OUT_F, HID), dtype=jnp.float32) * scale
        b2 = jax.random.normal(k4, (OUT_F,), dtype=jnp.float32) * scale
        return {'x': x, 'w1': w1, 'w2': w2, 'b2': b2, 'sparse_mask': make_sparse_mask()}
    _L0_attn_all = _L0_attn_setup()
    _L0_attn_in = {k: v for k, v in _L0_attn_all.items() if k in ('w1', 'w2', 'b2', 'sparse_mask')}
    del _L0_attn_all

    def _L0_xattn_setup():
        import jax, jax.numpy as jnp
        import numpy as np
        BS, SEQ, D_MODEL = (4, 128, 512)
        N_Q_HEADS, N_KV_HEADS, D_K, D_V = (32, 8, 128, 128)
        ROPE_BASE = 10000.0

        def _rotate_half(x):
            x1, x2 = jnp.split(x, 2, axis=-1)
            return jnp.concatenate([-x2, x1], axis=-1)

        def _apply_rope(x, pos0):
            d = x.shape[-1]
            seq = x.shape[2]
            inv_freq = 1.0 / ROPE_BASE ** (jnp.arange(0, d, 2, dtype=jnp.float32) / d)
            pos = (pos0 + jnp.arange(seq)).astype(jnp.float32)
            ang = pos[:, None] * inv_freq[None, :]
            cos = jnp.concatenate([jnp.cos(ang), jnp.cos(ang)], axis=-1)
            sin = jnp.concatenate([jnp.sin(ang), jnp.sin(ang)], axis=-1)
            return x * cos[None, None] + _rotate_half(x) * sin[None, None]
        key = jax.random.key(seed)
        ks = jax.random.split(key, 8)
        w_scale = 0.02
        return {'query': jax.random.normal(ks[0], (BS, SEQ, D_MODEL), dtype=jnp.float32), 'key': jax.random.normal(ks[1], (BS, SEQ, D_MODEL), dtype=jnp.float32), 'value': jax.random.normal(ks[2], (BS, SEQ, D_MODEL), dtype=jnp.float32), 'mask': jnp.zeros((BS, SEQ, SEQ), dtype=jnp.float32), 'wq': jax.random.normal(ks[3], (D_MODEL, N_Q_HEADS * D_K), dtype=jnp.float32) * w_scale, 'wk': jax.random.normal(ks[4], (D_MODEL, N_KV_HEADS * D_K), dtype=jnp.float32) * w_scale, 'wv': jax.random.normal(ks[5], (D_MODEL, N_KV_HEADS * D_V), dtype=jnp.float32) * w_scale, 'wo': jax.random.normal(ks[6], (N_Q_HEADS * D_V, D_MODEL), dtype=jnp.float32) * w_scale, 'curr_seq_pos': 0}
    _L0_xattn_all = _L0_xattn_setup()
    _L0_xattn_in = {k: v for k, v in _L0_xattn_all.items() if k in ('wq', 'wk', 'wv', 'wo')}
    del _L0_xattn_all

    def _L0_ffn_setup():
        import jax, jax.numpy as jnp
        import numpy as np
        LORA_SCALING = 1.0 / 2.0

        def _qlora_linear(x, wq, A, B):
            w = jnp.tile(wq, (1, 4))
            base = x @ w.T
            lora = x @ A.T @ B.T
            return base + lora * LORA_SCALING
        key = jax.random.key(seed)
        ks = jax.random.split(key, 10)
        d, h, r = (512, 1376, 2)
        return {'x': jax.random.normal(ks[0], (16, 1, d), dtype=jnp.float32), 'w1q': jax.random.normal(ks[1], (h, d // 4), dtype=jnp.float32) * 0.02, 'a1': jax.random.normal(ks[2], (r, d), dtype=jnp.float32) * 0.02, 'b1': jax.random.normal(ks[3], (h, r), dtype=jnp.float32) * 0.02, 'w3q': jax.random.normal(ks[4], (h, d // 4), dtype=jnp.float32) * 0.02, 'a3': jax.random.normal(ks[5], (r, d), dtype=jnp.float32) * 0.02, 'b3': jax.random.normal(ks[6], (h, r), dtype=jnp.float32) * 0.02, 'w2q': jax.random.normal(ks[7], (d, h // 4), dtype=jnp.float32) * 0.02, 'a2': jax.random.normal(ks[8], (r, h), dtype=jnp.float32) * 0.02, 'b2': jax.random.normal(ks[9], (d, r), dtype=jnp.float32) * 0.02}
    _L0_ffn_all = _L0_ffn_setup()
    _L0_ffn_in = {k: v for k, v in _L0_ffn_all.items() if k in ('w1q', 'a1', 'b1', 'w3q', 'a3', 'b3', 'w2q', 'a2', 'b2')}
    del _L0_ffn_all
    return {'x': x, 'ctx_4096': ctx_4096, 'mask_BxSxS2_ff0': mask_BxSxS2_ff0, 'L0_attn_w1': _L0_attn_in['w1'], 'L0_attn_w2': _L0_attn_in['w2'], 'L0_attn_b2': _L0_attn_in['b2'], 'L0_attn_sparse_mask': _L0_attn_in['sparse_mask'], 'L0_xattn_wq': _L0_xattn_in['wq'], 'L0_xattn_wk': _L0_xattn_in['wk'], 'L0_xattn_wv': _L0_xattn_in['wv'], 'L0_xattn_wo': _L0_xattn_in['wo'], 'L0_ffn_w1q': _L0_ffn_in['w1q'], 'L0_ffn_a1': _L0_ffn_in['a1'], 'L0_ffn_b1': _L0_ffn_in['b1'], 'L0_ffn_w3q': _L0_ffn_in['w3q'], 'L0_ffn_a3': _L0_ffn_in['a3'], 'L0_ffn_b3': _L0_ffn_in['b3'], 'L0_ffn_w2q': _L0_ffn_in['w2q'], 'L0_ffn_a2': _L0_ffn_in['a2'], 'L0_ffn_b2': _L0_ffn_in['b2']}

def reference(x, ctx_4096, mask_BxSxS2_ff0, L0_attn_w1, L0_attn_w2, L0_attn_b2, L0_attn_sparse_mask, L0_xattn_wq, L0_xattn_wk, L0_xattn_wv, L0_xattn_wo, L0_ffn_w1q, L0_ffn_a1, L0_ffn_b1, L0_ffn_w3q, L0_ffn_a3, L0_ffn_b3, L0_ffn_w2q, L0_ffn_a2, L0_ffn_b2):
    import jax
    import jax.numpy as jnp

    def _L0_attn_ref(x, w1, w2, b2, sparse_mask):
        import math
        import jax, jax.numpy as jnp
        import numpy as np
        IN_F, OUT_F, HID = (512, 512, 512)
        WINDOW, STRIPES = (6, 3)

        def make_sparse_mask(n_in=IN_F, n_out=OUT_F, window=WINDOW, stripes=STRIPES):
            m = np.zeros((n_in, n_out), dtype=np.float32)
            stride = int(math.sqrt(n_in))
            for k in range(stripes):
                ps = stride * k
                for i in range(0, n_in, window):
                    m[ps + i:ps + i + window, i:i + window] = 1.0
            mb = m.astype(bool)
            return jnp.asarray((mb | mb.T).astype(np.float32))
        attn = jnp.einsum('ds,td->st', w1, w2) * sparse_mask
        y = jnp.einsum('bds,st->bdt', x, attn) + b2
        return jax.nn.gelu(y, approximate=False)

    def _L0_xattn_ref(query, key, value, mask, wq, wk, wv, wo, curr_seq_pos):
        import jax, jax.numpy as jnp
        import numpy as np
        BS, SEQ, D_MODEL = (4, 128, 512)
        N_Q_HEADS, N_KV_HEADS, D_K, D_V = (32, 8, 128, 128)
        ROPE_BASE = 10000.0

        def _rotate_half(x):
            x1, x2 = jnp.split(x, 2, axis=-1)
            return jnp.concatenate([-x2, x1], axis=-1)

        def _apply_rope(x, pos0):
            d = x.shape[-1]
            seq = x.shape[2]
            inv_freq = 1.0 / ROPE_BASE ** (jnp.arange(0, d, 2, dtype=jnp.float32) / d)
            pos = (pos0 + jnp.arange(seq)).astype(jnp.float32)
            ang = pos[:, None] * inv_freq[None, :]
            cos = jnp.concatenate([jnp.cos(ang), jnp.cos(ang)], axis=-1)
            sin = jnp.concatenate([jnp.sin(ang), jnp.sin(ang)], axis=-1)
            return x * cos[None, None] + _rotate_half(x) * sin[None, None]
        bs, sq, _ = query.shape
        n_groups = N_Q_HEADS // N_KV_HEADS
        q = (query @ wq).reshape(bs, sq, N_Q_HEADS, D_K).transpose((0, 2, 1, 3))
        sk = key.shape[1]
        k = (key @ wk).reshape(bs, sk, N_KV_HEADS, 1, D_K)
        k = jnp.repeat(k, n_groups, axis=3).reshape(bs, sk, N_Q_HEADS, D_K).transpose((0, 2, 1, 3))
        v = (value @ wv).reshape(bs, sk, N_KV_HEADS, 1, D_V)
        v = jnp.repeat(v, n_groups, axis=3).reshape(bs, sk, N_Q_HEADS, D_V).transpose((0, 2, 1, 3))
        scale = jnp.sqrt(jnp.float32(D_K))
        q = _apply_rope(q, curr_seq_pos)
        k = _apply_rope(k, curr_seq_pos)
        raw = jnp.einsum('bhqd,bhkd->bhqk', q, k) / scale
        masked = raw + mask[:bs, None, curr_seq_pos:curr_seq_pos + sq, :sk]
        attn = jax.nn.softmax(masked, axis=-1)
        out = jnp.einsum('bhqk,bhkd->bhqd', attn, v)
        out = out.transpose((0, 2, 1, 3)).reshape(bs, sq, N_Q_HEADS * D_V)
        return out @ wo

    def _L0_ffn_ref(x, w1q, a1, b1, w3q, a3, b3, w2q, a2, b2):
        import jax, jax.numpy as jnp
        import numpy as np
        LORA_SCALING = 1.0 / 2.0

        def _qlora_linear(x, wq, A, B):
            w = jnp.tile(wq, (1, 4))
            base = x @ w.T
            lora = x @ A.T @ B.T
            return base + lora * LORA_SCALING
        gate = jax.nn.silu(_qlora_linear(x, w1q, a1, b1))
        up = _qlora_linear(x, w3q, a3, b3)
        return _qlora_linear(gate * up, w2q, a2, b2)
    x = x + _L0_attn_ref(_layernorm(x, axis=-1), L0_attn_w1, L0_attn_w2, L0_attn_b2, L0_attn_sparse_mask)
    x = x + _L0_xattn_ref(_layernorm(x, axis=-1), ctx_4096, ctx_4096, mask_BxSxS2_ff0, L0_xattn_wq, L0_xattn_wk, L0_xattn_wv, L0_xattn_wo, 0)
    x = x + _L0_ffn_ref(_layernorm(x, axis=-1), L0_ffn_w1q, L0_ffn_a1, L0_ffn_b1, L0_ffn_w3q, L0_ffn_a3, L0_ffn_b3, L0_ffn_w2q, L0_ffn_a2, L0_ffn_b2)
    return x

_drawn_inputs = setup_inputs


def setup_inputs(seed=0):
    import zlib

    import numpy as np

    out = dict(_drawn_inputs(seed))
    spreads = {}
    factors = {'L0_attn_b2': 2.707,
     'L0_xattn_wq': 3.308,
     'L0_xattn_wk': 3.313,
     'L0_ffn_a1': 8.0,
     'L0_ffn_b1': 8.0,
     'L0_ffn_a3': 8.0,
     'L0_ffn_b3': 8.0,
     'L0_ffn_a2': 8.0,
     'L0_ffn_b2': 8.0}
    for name, (base, spread) in spreads.items():
        noise = np.random.default_rng([zlib.crc32(name.encode()), seed]).standard_normal(out[name].shape)
        drawn = base * np.exp(spread * noise) if base else spread * noise
        out[name] = jnp.asarray(drawn.astype(out[name].dtype))
    for name, factor in factors.items():
        out[name] = (out[name] * factor).astype(out[name].dtype)
    return out
```

```python
from contextlib import ExitStack

import numpy as np

import concourse.bass as bass
from concourse import mybir

F32 = mybir.dt.float32
F32R = mybir.dt.float32r
ALU = mybir.AluOpType
ACT = mybir.ActivationFunctionType
AX = mybir.AxisListType

P = 128
B, S, D = 8, 128, 512
KC = D // P
TOK = B * S
HALF = TOK // 2
QH, KV, DK = 32, 8, 128
HG = QH // KV
FF = 1376
FQ = FF // 4
FT = (FQ + P - 1) // P
EPS = 1e-5
RANK = 2
STK = 96
LOWEST = -3.4e38

SLOTS = KV * B
TE = HG + 1
CH_A, CH_CTX, CH_G = 8, 8, 10
CH0 = CH_A + CH_CTX
NCH = CH0 + KV * CH_G
WK, WQ, WV, WO = 0, 1, 5, 6
RING = 4
FIRST, BODY = 2, 16
TURNS = 3
SPLIT_AT = [[0], [1], [2], [3], [4, 5], [6], [7], [8, 9]]


def tiles_of(n):
    if n == -1:
        return list(range(TE)) + [TE, TE + 1]
    half = (n + 5 - n % 4) // 4 if n % 4 != 3 else (n + 5) // 4
    half = {3: (n + 5) // 4, 0: (n + 4) // 4, 1: (n + 3) // 4, 2: (n + 2) // 4}[n % 4]
    if half >= 2 * KV:
        return []
    return [TE * half + e for e in {3: [0, 1], 0: [2], 1: [3], 2: [4]}[n % 4]]


def chunks_of(n):
    if n >= SLOTS - B:
        return []
    return [CH0 + CH_G * (n // B + 1) + i for i in SPLIT_AT[n % B]]


def decoder_block(nc, stream, x, mask, consts, spmask, b2, w1q, w3q, w2q, a_cols, bg_rows, bu_rows,
                  a2_cols, b2_rows, out):
    with ExitStack() as ctx:
        def sem(name):
            return ctx.enter_context(nc.semaphore(name))

        def sb(scope, name, shape, dt=F32):
            return scope.enter_context(nc.sbuf_tensor(name, shape, dt))

        ps = ctx.enter_context(nc.psum_tensor("ps", [P, 8, 512], F32))
        xres = sb(ctx, "xres", [P, B, D])
        maskq = sb(ctx, "maskq", [P, B, S])
        cst = sb(ctx, "cst", [P, 3 * P + 2 * STK + 16])
        stats = sb(ctx, "stats", [P, 2, 6])
        mv = sb(ctx, "mv", [P, 3, B, 2])
        vep = sb(ctx, "vep", [P, 3, B])
        rstd = sb(ctx, "rstd", [P, 3, B])
        mx = sb(ctx, "mx", [P, 2, HG])
        nmx = sb(ctx, "nmx", [P, 2, HG])
        rs = sb(ctx, "rs", [P, 2, HG])
        rc = sb(ctx, "rc", [P, 2, HG])
        ident = cst[:, 0:P]
        cosT, sinT = cst[:, P:2 * P], cst[:, 2 * P:3 * P]
        sel_raw = cst[:, 3 * P:3 * P + 2 * STK]
        minus_half = cst[:, 3 * P + 2 * STK:3 * P + 2 * STK + B]

        r1 = ExitStack()
        xT_h = sb(r1, "xT_h", [P, KC, TOK], F32R)
        xT_l = sb(r1, "xT_l", [P, KC, TOK], F32R)
        wq_h = sb(r1, "wq_h", [P, HG, KC, P], F32R)
        wq_l = sb(r1, "wq_l", [P, HG, KC, P], F32R)
        wk_h = sb(r1, "wk_h", [P, KC, P], F32R)
        wk_l = sb(r1, "wk_l", [P, KC, P], F32R)
        r2 = ExitStack()
        stg = sb(r2, "stg", [P, RING, 512])
        cT_h = sb(r2, "cT_h", [P, KC, TOK], F32R)
        cT_l = sb(r2, "cT_l", [P, KC, TOK], F32R)
        wv_h = sb(r2, "wv_h", [P, 2, KC, P], F32R)
        wv_l = sb(r2, "wv_l", [P, 2, KC, P], F32R)
        r3 = ExitStack()
        w1_h = sb(r3, "w1_h", [P, KC, D], F32R)
        w1_l = sb(r3, "w1_l", [P, KC, D], F32R)
        w2_h = sb(r3, "w2_h", [P, KC, D], F32R)
        w2_l = sb(r3, "w2_l", [P, KC, D], F32R)
        at_h = sb(r3, "at_h", [P, KC, D], F32R)
        at_l = sb(r3, "at_l", [P, KC, D], F32R)
        atf = sb(r3, "atf", [P, 2, D])
        spm = sb(r3, "spm", [P, KC, D])
        xn = sb(r3, "xn", [P, 2, D])
        yb = sb(r3, "yb", [P, 2, D])
        b2b = sb(r3, "b2b", [P, D])
        r3.close()
        r3 = ExitStack()
        wo_h = sb(r3, "wo_h", [P, 2, HG, 512], F32R)
        wo_l = sb(r3, "wo_l", [P, 2, HG, 512], F32R)
        qr = sb(r3, "qr", [P, 2, TE, HALF])
        qs_h = sb(r3, "qs_h", [P, 2, TE, P], F32R)
        qs_l = sb(r3, "qs_l", [P, 2, TE, P], F32R)
        rot = sb(r3, "rot", [P, 2, HALF])
        pr = sb(r3, "pr", [P, 2, HG, P])
        pT_h = sb(r3, "pT_h", [P, HG * P], F32R)
        pT_l = sb(r3, "pT_l", [P, HG * P], F32R)
        o_h = sb(r3, "o_h", [P, HG * P], F32R)
        o_l = sb(r3, "o_l", [P, HG * P], F32R)
        v_h = sb(r3, "v_h", [P, 2, P], F32R)
        v_l = sb(r3, "v_l", [P, 2, P], F32R)
        r3.close()
        r2.close()
        r1.close()
        r1 = ExitStack()
        g1_h = sb(r1, "g1_h", [P, FF], F32R)
        g1_l = sb(r1, "g1_l", [P, FF], F32R)
        g3_h = sb(r1, "g3_h", [P, FF], F32R)
        g3_l = sb(r1, "g3_l", [P, FF], F32R)
        g1_raw = sb(r1, "g1_raw", [P, FF])
        g3_raw = sb(r1, "g3_raw", [P, FF])
        a_raw = sb(r1, "a_raw", [P, KC, STK])
        a_h = sb(r1, "a_h", [P, KC, STK], F32R)
        a_l = sb(r1, "a_l", [P, KC, STK], F32R)
        bg_s = sb(r1, "bg_s", [STK, FF], F32R)
        pad1 = sb(r1, "pad1", [P, 52 * 256 - (5 * FF + 2 * FF) - 3 * KC * STK])
        r2 = ExitStack()
        bg_raw = sb(r2, "bg_raw", [STK, FF])
        bu_raw = sb(r2, "bu_raw", [STK, FF])
        bu_s = sb(r2, "bu_s", [STK, FF], F32R)
        g2_raw = sb(r2, "g2_raw", [P, FT, D])
        g2_h = sb(r2, "g2_h", [P, FT, D], F32R)
        g2_l = sb(r2, "g2_l", [P, FT, D], F32R)
        bd_raw = sb(r2, "bd_raw", [STK, D])
        bd_s = sb(r2, "bd_s", [STK, D], F32R)
        xs_h = sb(r2, "xs_h", [P, TOK], F32R)
        pad2 = sb(r2, "pad2", [P, 48 * 256 - 3 * FF - 3 * FT * D - 2 * D - TOK])
        r3 = ExitStack()
        xs_l = sb(r3, "xs_l", [P, TOK], F32R)
        xs_f = sb(r3, "xs_f", [P, TOK])
        xn3 = sb(r3, "xn3", [P, 2, D])
        xc_h = sb(r3, "xc_h", [P, KC, HALF], F32R)
        xc_l = sb(r3, "xc_l", [P, KC, HALF], F32R)
        u_s = sb(r3, "u_s", [STK, TOK], F32R)
        gsum = sb(r3, "gsum", [P, FT, HALF])
        gs_h = sb(r3, "gs_h", [P, FT, HALF], F32R)
        gs_l = sb(r3, "gs_l", [P, FT, HALF], F32R)
        a2c = sb(r3, "a2c", [P, FT * 4, RANK])
        lacc = sb(r3, "lacc", [P, RANK, HALF])
        lo_h = sb(r3, "lo_h", [P, RANK, HALF], F32R)
        lo_l = sb(r3, "lo_l", [P, RANK, HALF], F32R)
        sil = sb(r3, "sil", [P, 2, HALF])
        gate = sb(r3, "gate", [P, 2, HALF])
        v_s = sb(r3, "v_s", [STK, HALF], F32R)
        sel = sb(r3, "sel", [P, RANK, STK], F32R)
        ost = sb(r3, "ost", [P, 2, D])
        r3.close()
        r2.close()
        r1.close()
        del pad1, pad2

        in_cst, in_b2, in_spm, in_mask = sem("in_cst"), sem("in_b2"), sem("in_spm"), sem("in_mask")
        in_x = [sem(f"in_x{b}") for b in range(B)]
        in_stg = [sem(f"in_stg{r}") for r in range(RING)]
        chunk_hi, chunk_lo, wlo = sem("chunk_hi"), sem("chunk_lo"), sem("wlo")
        agg, vepd, powd, xnd = sem("agg"), sem("vepd"), sem("powd"), sem("xnd")
        bns = sem("bns")
        wprod, attd, at_hid, at_lod = sem("wprod"), sem("attd"), sem("at_hid"), sem("at_lod")
        tr, tr_hi, tr_lo = sem("tr"), sem("tr_hi"), sem("tr_lo")
        ymm, ybd, gel, x1d = sem("ymm"), sem("ybd"), sem("gel"), sem("x1d")
        tile_mm, rope_mul, rope_add = sem("tile_mm"), sem("rope_mul"), sem("rope_add")
        q_hi, q_lo = sem("q_hi"), sem("q_lo")
        scored, masked, maxed, expd, recd, normd = (sem("scored"), sem("masked"), sem("maxed"),
                                                    sem("expd"), sem("recd"), sem("normd"))
        pT, pT_hid, pT_lod = sem("pT"), sem("pT_hid"), sem("pT_lod")
        vmm, v_hid, v_lod = sem("vmm"), sem("v_hid"), sem("v_lod")
        pv, o_hid, o_lod = sem("pv"), sem("o_hid"), sem("o_lod")
        womm, accd = sem("womm"), sem("accd")
        in_ff, in_ff2, cz = sem("in_ff"), sem("in_ff2"), sem("cz")
        cw_hi, cw_lo = sem("cw_hi"), sem("cw_lo")
        t3, t3_hi, t3_lo, xsum = sem("t3"), sem("t3_hi"), sem("t3_lo"), sem("xsum")
        xs_hid, xs_lod = sem("xs_hid"), sem("xs_lod")
        umm, u_hid, u_lod = sem("umm"), sem("u_hid"), sem("u_lod")
        gu, sild, gated, gsd, gs_hid, gs_lod = (sem("gu"), sem("sild"), sem("gated"), sem("gsd"),
                                                sem("gs_hid"), sem("gs_lod"))
        lod, l_hid, l_lod, vm, v3_hi, v3_lo = (sem("lod"), sem("l_hid"), sem("l_lod"), sem("vm"),
                                               sem("v3_hi"), sem("v3_lo"))
        down, outd, stored = sem("down"), sem("outd"), [sem("stored0"), sem("stored1")]

        def three(pe, dst, a_hi, a_lo, b_hi, b_lo, first, last):
            pe.matmul(dst, a_hi, b_hi, start=first, stop=False)
            pe.matmul(dst, a_hi, b_lo, start=False, stop=False)
            return pe.matmul(dst, a_lo, b_hi, start=False, stop=last)

        def f(ap):
            return ap.bitcast(F32)

        def at(value, per_turn, turn):
            return value if turn is None else turn * per_turn + value

        def chunk_dst(c):
            if c < CH_A:
                return (w2_h, w2_l)[0][:, c // 2] if c % 2 else w1_h[:, c // 2], \
                    w2_l[:, c // 2] if c % 2 else w1_l[:, c // 2]
            if c < CH0:
                k, hf = (c - CH_A) // 2, (c - CH_A) % 2
                cols = slice(hf * HALF, (hf + 1) * HALF)
                return cT_h[:, k, cols], cT_l[:, k, cols]
            g, i = (c - CH0) // CH_G, (c - CH0) % CH_G
            if i == WK:
                pair = wk_h[:], wk_l[:]
            elif i < WV:
                pair = wq_h[:, i - WQ], wq_l[:, i - WQ]
            elif i == WV:
                pair = wv_h[:, g % 2], wv_l[:, g % 2]
            else:
                return wo_h[:, g % 2, i - WO], wo_l[:, g % 2, i - WO]
            return tuple(p.rearrange("p k c -> p (k c)") for p in pair)

        turns_a = [(1, 0), (1, 1)]
        for b in range(B + 2):
            turns_a += [(1, b + 2)] * (b + 2 < B) + [(2, b - 2)] * (b >= 2)
        place_a = {t: i for i, t in enumerate(turns_a)}
        PRE = 18

        loop_slots = range(FIRST, FIRST + BODY)
        tail_slots = range(FIRST + BODY * TURNS, SLOTS + 2)
        TPT, CPT = TE * BODY // 4, CH_G * BODY // B

        block = ctx.enter_context(nc.Block())

        @block.sync
        def _(sp):
            def load_chunk(c, turn=None, src=None):
                if c >= RING:
                    if c - RING < CH_A:
                        sp.wait_ge(wlo, c - RING + 1)
                    else:
                        sp.wait_ge(chunk_lo, at(c - RING - CH_A + 1, RING, turn))
                sp.dma_start(stg[:, c % RING, :], stream[c] if src is None else src)\
                  .then_inc(in_stg[c % RING], 16)

            for c in range(RING):
                load_chunk(c)
            sp.dma_start(cst[:], consts).then_inc(in_cst, 16)
            for b in range(2):
                sp.dma_start(xres[:, b, :], x[b]).then_inc(in_x[b], 16)
            for c in range(RING, CH_A):
                load_chunk(c)
            sp.dma_start(spm[:], spmask.rearrange("(m p) t -> p m t", p=P)).then_inc(in_spm, 16)
            for b in range(2, B):
                sp.dma_start(xres[:, b, :], x[b]).then_inc(in_x[b], 16)
            sp.dma_start(b2b[:], b2.rearrange("(a t) -> a t", a=1).to_broadcast([P, D]))\
              .then_inc(in_b2, 16)
            sp.dma_start(maskq[:], mask.rearrange("b q k -> q b k")).then_inc(in_mask, 16)
            for c in range(CH_A, 4 * RING):
                load_chunk(c)
            with sp.Fori(0, (NCH - 4 * RING) // RING) as turn:
                for r in range(RING):
                    place = sp.snap(turn * RING + (4 * RING + r))
                    load_chunk(4 * RING + r, turn, stream[bass.ds(place, 1)].rearrange("a p n -> (a p) n"))
            sp.wait_ge(tile_mm, TE * 2 * KV)
            sp.dma_start(g1_raw[:], w1q).then_inc(in_ff, 16)
            sp.dma_start(g3_raw[:], w3q).then_inc(in_ff, 16)
            sp.dma_start(a_raw[:], a_cols.rearrange("(k p) c -> p k c", p=P)).then_inc(in_ff, 16)
            sp.wait_ge(vmm, SLOTS)
            sp.wait_ge(chunk_hi, NCH)
            sp.wait_ge(chunk_lo, NCH - CH_A)
            sp.dma_start(bg_raw[:], bg_rows).then_inc(in_ff2, 16)
            sp.dma_start(bu_raw[:], bu_rows).then_inc(in_ff2, 16)
            sp.dma_start(g2_raw[:, 0:FT - 1, :], w2q[0:(FT - 1) * P].rearrange("(t p) n -> p t n", p=P))\
              .then_inc(in_ff2, 16)
            sp.dma_start(g2_raw[0:FQ - (FT - 1) * P, FT - 1, :], w2q[(FT - 1) * P:FQ]).then_inc(in_ff2, 16)
            sp.dma_start(bd_raw[:], b2_rows).then_inc(in_ff2, 16)
            sp.wait_ge(accd, SLOTS)
            sp.dma_start(a2c[:], a2_cols).then_inc(in_ff2, 16)
            for b in range(B):
                sp.wait_ge(outd, b + 1)
                sp.dma_start(out[b], ost[:, b % 2, :]).then_inc(stored[b % 2], 16)
            for r in range(2):
                sp.wait_ge(stored[r], 16 * B // 2)

        @block.tensor
        def _(pe):
            for k in range(KC):
                pe.wait_ge(chunk_hi, 2 * k + 2)
                pe.wait_ge(wlo, 2 * k + 2)
                for m in range(KC):
                    cols = slice(m * P, (m + 1) * P)
                    mm = three(pe, ps[:, m, :], w1_h[:, k, cols], w1_l[:, k, cols],
                               w2_h[:, k, :], w2_l[:, k, :], k == 0, k == KC - 1)
                    if k == KC - 1:
                        mm.then_inc(wprod, 1)

            def transpose_a(norm, b):
                i = place_a[norm, b]
                pe.wait_ge(xnd, i + 1)
                if i >= 2:
                    pe.wait_ge(tr_lo, i - 1)
                for k in range(KC):
                    mm = pe.transpose(ps[:, 4 + i % 2, k * P:(k + 1) * P],
                                      xn[:, i % 2, k * P:(k + 1) * P], ident)
                mm.then_inc(tr, 1)

            pe.wait_ge(in_cst, 16)
            transpose_a(1, 0)
            transpose_a(1, 1)
            for b in range(B + 2):
                if b < B:
                    if b == 0:
                        pe.wait_ge(at_lod, KC)
                    pe.wait_ge(tr_lo, place_a[1, b] + 1)
                    if b >= 2:
                        pe.wait_ge(ybd, b - 1)
                    cols = slice(b * S, (b + 1) * S)
                    for k in range(KC):
                        mm = three(pe, ps[:, 6 + b % 2, :], xT_h[:, k, cols], xT_l[:, k, cols],
                                   at_h[:, k, :], at_l[:, k, :], k == 0, k == KC - 1)
                    mm.then_inc(ymm, 1)
                if b + 2 < B:
                    transpose_a(1, b + 2)
                if b >= 2:
                    transpose_a(2, b - 2)

            def project(t, turn):
                half, e = t // TE, t % TE
                g = half // 2
                pe.wait_ge(chunk_lo, at(CH0 + CH_G * g + e - CH_A + 1, CPT, turn))
                if t < 2 * TE:
                    pe.wait_ge(tr_lo, place_a[2, 4 * half + 3] + 1)
                if t >= 2:
                    pe.wait_ge(rope_mul, at(t - 1, TPT, turn))
                cols = slice((half % 2) * HALF, (half % 2 + 1) * HALF)
                for k in range(KC):
                    if e == 0:
                        mm = three(pe, ps[:, 2 + t % 2, :], wk_h[:, k, :], wk_l[:, k, :],
                                   cT_h[:, k, cols], cT_l[:, k, cols], k == 0, k == KC - 1)
                    else:
                        mm = three(pe, ps[:, 2 + t % 2, :], wq_h[:, e - 1, k, :], wq_l[:, e - 1, k, :],
                                   xT_h[:, k, cols], xT_l[:, k, cols], k == 0, k == KC - 1)
                mm.then_inc(tile_mm, 1)

            def slot(n, turn=None):
                b, g = n % B, n // B
                if n < SLOTS:
                    pe.wait_ge(q_lo, at(n + 1, BODY, turn))
                    if n >= 2:
                        pe.wait_ge(masked, at(n - 1, BODY, turn))
                    for h in range(HG):
                        mm = three(pe, ps[:, n % 2, h * P:(h + 1) * P],
                                   qs_h[:, n % 2, 1 + h, :], qs_l[:, n % 2, 1 + h, :],
                                   qs_h[:, n % 2, 0, :], qs_l[:, n % 2, 0, :], True, True)
                    mm.then_inc(scored, 1)
                for t in tiles_of(n):
                    project(t, turn)
                if 1 <= n <= SLOTS:
                    pe.wait_ge(normd, at(n, BODY, turn))
                    if n >= 2:
                        pe.wait_ge(pT_lod, at(n - 1, BODY, turn))
                    for h in range(HG):
                        mm = pe.transpose(ps[:, 4, h * P:(h + 1) * P], pr[:, (n - 1) % 2, h, :], ident)
                    mm.then_inc(pT, 1)
                if n >= 2:
                    m = n - 2
                    pe.wait_ge(o_lod, at(m + 1, BODY, turn))
                    pe.wait_ge(chunk_lo, at(CH0 + CH_G * (m // B) + CH_G - CH_A, CPT, turn))
                    if m >= 1:
                        pe.wait_ge(accd, at(m, BODY, turn))
                    for h in range(HG):
                        cols = slice(h * P, (h + 1) * P)
                        mm = three(pe, ps[:, 6, :], o_h[:, cols], o_l[:, cols],
                                   wo_h[:, (m // B) % 2, h, :], wo_l[:, (m // B) % 2, h, :],
                                   h == 0, h == HG - 1)
                    mm.then_inc(womm, 1)
                if n < SLOTS:
                    pe.wait_ge(chunk_lo, at(CH0 + CH_G * g + WV - CH_A + 1, CPT, turn))
                    if n >= 1:
                        pe.wait_ge(v_lod, at(n, BODY, turn))
                    cols = slice(b * S, (b + 1) * S)
                    for k in range(KC):
                        mm = three(pe, ps[:, 7, 0:P], cT_h[:, k, cols], cT_l[:, k, cols],
                                   wv_h[:, g % 2, k, :], wv_l[:, g % 2, k, :], k == 0, k == KC - 1)
                    mm.then_inc(vmm, 1)
                if 1 <= n <= SLOTS:
                    m = n - 1
                    pe.wait_ge(pT_lod, at(m + 1, BODY, turn))
                    pe.wait_ge(v_lod, at(m + 1, BODY, turn))
                    if m >= 1:
                        pe.wait_ge(o_lod, at(m, BODY, turn))
                    three(pe, ps[:, 5, :], v_h[:, m % 2, :], v_l[:, m % 2, :],
                          pT_h[:], pT_l[:], True, True).then_inc(pv, 1)

            for t in tiles_of(-1):
                project(t, None)
            for n in range(FIRST):
                slot(n)
            with pe.Fori(0, TURNS) as turn:
                for n in loop_slots:
                    slot(n, turn)
            for n in tail_slots:
                slot(n)

            def transpose_c(b):
                pe.wait_ge(xnd, len(turns_a) + b + 1)
                if b >= 2:
                    pe.wait_ge(xsum, b - 1)
                for k in range(KC):
                    mm = pe.transpose(ps[:, 4 + b % 2, k * P:(k + 1) * P],
                                      xn3[:, b % 2, k * P:(k + 1) * P], ident)
                mm.then_inc(t3, 1)

            def lora_in(hf):
                if hf == 0:
                    pe.wait_ge(cw_lo, 1)
                pe.wait_ge(t3_lo, 4 * hf + 4)
                for k in range(KC):
                    mm = three(pe, ps[0:STK, 6 + hf, :], a_h[:, k, :], a_l[:, k, :],
                               xc_h[:, k, :], xc_l[:, k, :], k == 0, k == KC - 1)
                mm.then_inc(umm, 1)

            def up(hf, t, j):
                i = hf * FT * 4 + t * 4 + j
                rows = min(P, FQ - t * P)
                cols = slice(j * FQ + t * P, j * FQ + t * P + rows)
                toks = slice(hf * HALF, (hf + 1) * HALF)
                if i == 0:
                    pe.wait_ge(cw_lo, 5)
                if t == 0 and j == 0:
                    pe.wait_ge(xs_lod, hf + 1)
                    pe.wait_ge(u_lod, hf + 1)
                if i >= 2:
                    pe.wait_ge(gated, i - 1)
                for s, (w_h, w_l, rows_s) in enumerate(((g1_h, g1_l, bg_s), (g3_h, g3_l, bu_s))):
                    dst = ps[0:rows, 2 * s + i % 2, :]
                    three(pe, dst, w_h[:, cols], w_l[:, cols], xs_h[:, toks], xs_l[:, toks], True, False)
                    mm = pe.matmul(dst, rows_s[:, cols], u_s[:, toks], start=False, stop=True)
                mm.then_inc(gu, 1)

            def lora_out(hf):
                pe.wait_ge(l_lod, hf + 1)
                if hf == 1:
                    pe.wait_ge(v3_lo, 1)
                for r in range(RANK):
                    pe.matmul(ps[0:STK, 6, :], sel[:, r, :], lo_h[:, r, :], start=(r == 0), stop=False)
                    mm = pe.matmul(ps[0:STK, 6, :], sel[:, r, :], lo_l[:, r, :], start=False,
                                   stop=(r == RANK - 1))
                mm.then_inc(vm, 1)

            def down_c(b):
                hf = b // 4
                pe.wait_ge(v3_lo, hf + 1)
                pe.wait_ge(gs_lod, FT * hf + FT)
                if b == 0:
                    pe.wait_ge(cw_lo, 7)
                if b >= 2:
                    pe.wait_ge(outd, b - 1)
                bank = (5, 7)[b % 2]
                cols = slice((b % 4) * S, (b % 4 + 1) * S)
                for t in range(FT):
                    rows = min(P, FQ - t * P)
                    three(pe, ps[:, bank, :], gs_h[0:rows, t, cols], gs_l[0:rows, t, cols],
                          g2_h[0:rows, t, :], g2_l[0:rows, t, :], t == 0, False)
                pe.matmul(ps[:, bank, :], v_s[:, cols], bd_s[:], start=False, stop=True).then_inc(down, 1)

            for b in range(4):
                transpose_c(b)
            lora_in(0)
            for b in range(4, B):
                transpose_c(b)
            lora_in(1)
            for i in range(FT * 4):
                up(0, i // 4, i % 4)
            up(1, 0, 0)
            up(1, 0, 1)
            lora_out(0)
            for b in range(4):
                down_c(b)
            for i in range(2, FT * 4):
                up(1, i // 4, i % 4)
            lora_out(1)
            for b in range(4, B):
                down_c(b)

        @block.scalar
        def _(act):
            def chunk(c, turn=None):
                act.wait_ge(in_stg[c % RING], at(16 * (c // RING + 1), 16 * CPT // RING, turn))
                if c >= CH0 + CH_G:
                    g, i = (c - CH0) // CH_G, (c - CH0) % CH_G
                    if i < WV:
                        act.wait_ge(tile_mm, at(TE * (2 * g - 1) + i + 1, TPT, turn))
                    elif g >= 2 and i == WV:
                        act.wait_ge(vmm, at(B * (g - 1), BODY, turn))
                    elif g >= 2:
                        act.wait_ge(womm, at(B * (g - 1), BODY, turn))
                elif c >= CH0 + WO:
                    act.wait_ge(wprod, KC)
                act.copy(chunk_dst(c)[0], stg[:, c % RING, :]).then_inc(chunk_hi, 1)

            for c in range(CH_A):
                chunk(c)
            for m in range(KC):
                act.wait_ge(attd, m + 1)
                act.copy(at_h[:, m, :], atf[:, m % 2, :]).then_inc(at_hid, 1)

            def split_a(norm, b):
                i = place_a[norm, b]
                act.wait_ge(tr, i + 1)
                act.copy(xT_h[:, :, b * S:(b + 1) * S],
                         ps[:, 4 + i % 2, :].rearrange("p (k t) -> p k t", k=KC)).then_inc(tr_hi, 1)

            split_a(1, 0)
            split_a(1, 1)
            for b in range(B + 2):
                if b < B:
                    act.wait_ge(ybd, b + 1)
                    act.activation(yb[:, b % 2, :], yb[:, b % 2, :], ACT.Gelu).then_inc(gel, 1)
                if b + 2 < B:
                    split_a(1, b + 2)
                if b >= 2:
                    split_a(2, b - 2)
                if b < PRE // 2:
                    chunk(CH_A + 2 * b)
                    chunk(CH_A + 2 * b + 1)

            def split_q(n, turn):
                act.wait_ge(rope_add, at(TE * (n // 4) + TE, TPT, turn))
                if n >= 2:
                    act.wait_ge(scored, at(n - 1, BODY, turn))
                act.copy(qs_h[:, n % 2], qr[:, (n // 4) % 2, :, (n % 4) * P:(n % 4 + 1) * P])\
                   .then_inc(q_hi, 1)

            def slot(n, turn=None):
                if n >= 2:
                    m = n - 2
                    act.wait_ge(pv, at(m + 1, BODY, turn))
                    if m >= 1:
                        act.wait_ge(womm, at(m, BODY, turn))
                    act.copy(o_h[:], ps[:, 5, :]).then_inc(o_hid, 1)
                if n < SLOTS:
                    act.wait_ge(maxed, at(n + 1, BODY, turn))
                    for h in range(HG):
                        last = act.activation(pr[:, n % 2, h, :], pr[:, n % 2, h, :], ACT.Exp,
                                              bias=nmx[:, n % 2, h:h + 1], scale=1.0,
                                              accum_out=rs[:, n % 2, h:h + 1])
                    last.then_inc(expd, 1)
                for c in chunks_of(n):
                    chunk(c, turn)
                if 1 <= n <= SLOTS:
                    act.wait_ge(pT, at(n, BODY, turn))
                    if n >= 2:
                        act.wait_ge(pv, at(n - 1, BODY, turn))
                    act.copy(pT_h[:], ps[:, 4, :]).then_inc(pT_hid, 1)
                if n + 1 < SLOTS:
                    split_q(n + 1, turn)
                if n < SLOTS:
                    act.wait_ge(vmm, at(n + 1, BODY, turn))
                    if n >= 2:
                        act.wait_ge(pv, at(n - 1, BODY, turn))
                    act.copy(v_h[:, n % 2, :], ps[:, 7, 0:P]).then_inc(v_hid, 1)

            split_q(0, None)
            for n in range(FIRST):
                slot(n)
            with act.Fori(0, TURNS) as turn:
                for n in loop_slots:
                    slot(n, turn)
            for n in tail_slots:
                slot(n)

            act.wait_ge(in_ff, 3 * 16)
            act.wait_ge(tile_mm, TE * 2 * KV)
            act.copy(a_h[:], a_raw[:]).then_inc(cw_hi, 1)
            act.copy(g1_h[:], g1_raw[:]).then_inc(cw_hi, 1)
            act.copy(g3_h[:], g3_raw[:]).then_inc(cw_hi, 1)
            act.wait_ge(accd, SLOTS)
            act.wait_ge(in_ff2, 6 * 16)
            act.mul(bg_s[:], bg_raw[:], 0.5).then_inc(cw_hi, 1)
            act.mul(bu_s[:], bu_raw[:], 0.5).then_inc(cw_hi, 1)
            for b in range(4):
                act.wait_ge(t3, b + 1)
                act.copy(xc_h[:, :, b * S:(b + 1) * S],
                         ps[:, 4 + b % 2, :].rearrange("p (k t) -> p k t", k=KC)).then_inc(t3_hi, 1)

            def split_sum(hf):
                act.wait_ge(xsum, 4 * hf + 4)
                act.copy(xs_h[:, hf * HALF:(hf + 1) * HALF], xs_f[:, hf * HALF:(hf + 1) * HALF])\
                   .then_inc(xs_hid, 1)
                act.wait_ge(umm, hf + 1)
                act.copy(u_s[:, hf * HALF:(hf + 1) * HALF], ps[0:STK, 6 + hf, :]).then_inc(u_hid, 1)

            split_sum(0)
            for b in range(4, B):
                act.wait_ge(t3, b + 1)
                act.wait_ge(umm, 1)
                act.copy(xc_h[:, :, (b - 4) * S:(b - 3) * S],
                         ps[:, 4 + b % 2, :].rearrange("p (k t) -> p k t", k=KC)).then_inc(t3_hi, 1)
            split_sum(1)
            act.copy(g2_h[:, 0:FT - 1, :], g2_raw[:, 0:FT - 1, :])
            act.copy(g2_h[0:FQ - (FT - 1) * P, FT - 1, :], g2_raw[0:FQ - (FT - 1) * P, FT - 1, :])\
               .then_inc(cw_hi, 1)
            act.mul(bd_s[:], bd_raw[:], 0.5).then_inc(cw_hi, 1)
            act.copy(sel[:], sel_raw.rearrange("p (r c) -> p r c", r=RANK)).then_inc(cw_hi, 1)

            def silu(hf, t, j):
                i = hf * FT * 4 + t * 4 + j
                rows = min(P, FQ - t * P)
                act.wait_ge(gu, i + 1)
                if i >= 2:
                    act.wait_ge(gated, i - 1)
                act.activation(sil[0:rows, i % 2, :], ps[0:rows, i % 2, :], ACT.Silu).then_inc(sild, 1)

            def split_gs(hf, t):
                rows = min(P, FQ - t * P)
                act.wait_ge(gsd, (hf * FT + t + 1) * 3)
                if hf == 1:
                    act.wait_ge(down, 4)
                act.copy(gs_h[0:rows, t, :], gsum[0:rows, t, :]).then_inc(gs_hid, 1)

            def split_lora(hf):
                act.wait_ge(lod, (hf + 1) * FT * 4 * RANK)
                if hf == 1:
                    act.wait_ge(vm, 1)
                act.copy(lo_h[:], lacc[:]).then_inc(l_hid, 1)

            def split_v(hf):
                act.wait_ge(vm, hf + 1)
                if hf == 1:
                    act.wait_ge(down, 4)
                act.copy(v_s[:], ps[0:STK, 6, :]).then_inc(v3_hi, 1)

            for hf in range(2):
                for t in range(FT):
                    for j in range(4):
                        silu(hf, t, j)
                        if hf == 1 and t == 0 and j == 0:
                            split_gs(0, FT - 1)
                            split_lora(0)
                        if hf == 1 and t == 0 and j == 1:
                            split_v(0)
                        if t >= 1 and j == 0:
                            split_gs(hf, t - 1)
            split_gs(1, FT - 1)
            split_lora(1)
            split_v(1)

        @block.vector
        def _(dve):
            def norm_stats(norm, b):
                i = norm * B + b
                if i >= 2:
                    dve.wait_ge(agg, i - 1)
                dve.bn_stats(stats[:, i % 2, :], xres[:, b, :]).then_inc(bns, 1)
                dve.wait_ge(bns, i + 1)
                dve.bn_aggr(mv[:, norm, b, :], stats[:, i % 2, :]).then_inc(agg, 1)
                dve.wait_ge(agg, i + 1)
                dve.tensor_scalar(vep[:, norm, b:b + 1], mv[:, norm, b, 1:2], EPS, None, ALU.add)\
                   .then_inc(vepd, 1)

            def apply_norm(dst, norm, b):
                return dve.tensor_scalar(dst, xres[:, b, :], mv[:, norm, b, 0:1],
                                         rstd[:, norm, b:b + 1], ALU.subtract, ALU.mult)

            def norm_a(norm, b):
                i = place_a[norm, b]
                dve.wait_ge(powd, 1 if norm == 1 else b + 2)
                if i >= 2:
                    dve.wait_ge(tr, i - 1)
                apply_norm(xn[:, i % 2, :], norm - 1, b).then_inc(xnd, 1)

            def split_a(norm, b):
                i = place_a[norm, b]
                cols = slice(b * S, (b + 1) * S)
                dve.wait_ge(tr_hi, i + 1)
                dve.tensor_tensor(xT_l[:, :, cols], ps[:, 4 + i % 2, :].rearrange("p (k t) -> p k t", k=KC),
                                  f(xT_h[:, :, cols]), ALU.subtract).then_inc(tr_lo, 1)

            for c in range(CH_A):
                dve.wait_ge(chunk_hi, c + 1)
                hi, lo = chunk_dst(c)
                dve.tensor_tensor(lo, stg[:, c % RING, :], f(hi), ALU.subtract).then_inc(wlo, 1)
            for b in range(B):
                dve.wait_ge(in_x[b], 16)
                norm_stats(0, b)
            norm_a(1, 0)
            norm_a(1, 1)
            dve.wait_ge(in_spm, 16)
            for m in range(KC):
                dve.wait_ge(wprod, m + 1)
                if m >= 2:
                    dve.wait_ge(at_lod, m - 1)
                dve.tensor_tensor(atf[:, m % 2, :], ps[:, m, :], spm[:, m, :], ALU.mult).then_inc(attd, 1)
                dve.wait_ge(at_hid, m + 1)
                dve.tensor_tensor(at_l[:, m, :], atf[:, m % 2, :], f(at_h[:, m, :]), ALU.subtract)\
                   .then_inc(at_lod, 1)
            split_a(1, 0)
            split_a(1, 1)
            dve.wait_ge(in_b2, 16)
            for b in range(B + 2):
                if b + 2 < B:
                    norm_a(1, b + 2)
                if b < B:
                    dve.wait_ge(ymm, b + 1)
                    if b >= 2:
                        dve.wait_ge(x1d, b - 1)
                    dve.tensor_tensor(yb[:, b % 2, :], ps[:, 6 + b % 2, :], b2b[:], ALU.add).then_inc(ybd, 1)
                if 1 <= b <= B:
                    dve.wait_ge(x1d, b)
                    norm_stats(1, b - 1)
                if b >= 2:
                    norm_a(2, b - 2)
                if b + 2 < B:
                    split_a(1, b + 2)
                if b >= 2:
                    split_a(2, b - 2)

            def rope(t, turn):
                half, e = t // TE, t % TE
                dve.wait_ge(tile_mm, at(t + 1, TPT, turn))
                if half >= 2:
                    dve.wait_ge(q_lo, at(4 * half - 4, BODY, turn))
                if t >= 2:
                    dve.wait_ge(rope_add, at(t - 1, TPT, turn))
                src = ps[:, 2 + t % 2, :].rearrange("p (b s) -> p b s", b=4)
                dst = rot[:, t % 2, :].rearrange("p (b s) -> p b s", b=4)
                h = DK // 2

                def table(lo, hi, tab):
                    return tab[lo:hi, :].rearrange("p (a s) -> p a s", a=1).to_broadcast([hi - lo, 4, S])
                dve.tensor_tensor(qr[:, half % 2, e, :].rearrange("p (b s) -> p b s", b=4), src,
                                  table(0, DK, cosT), ALU.mult)
                dve.tensor_tensor(dst[0:h], src[h:DK], table(h, DK, sinT), ALU.mult)
                dve.tensor_tensor(dst[h:DK], src[0:h], table(0, h, sinT), ALU.mult).then_inc(rope_mul, 1)

            def slot(n, turn=None):
                b = n % B
                if n >= 2:
                    dve.wait_ge(o_hid, at(n - 1, BODY, turn))
                if n < SLOTS:
                    if n >= 2:
                        dve.wait_ge(pT, at(n - 1, BODY, turn))
                    dve.wait_ge(scored, at(n + 1, BODY, turn))
                if n >= 2:
                    dve.tensor_tensor(o_l[:], ps[:, 5, :], f(o_h[:]), ALU.subtract).then_inc(o_lod, 1)
                if n < SLOTS:
                    for h in range(HG):
                        last = dve.tensor_tensor_reduce(pr[:, n % 2, h, :], ps[:, n % 2, h * P:(h + 1) * P],
                                                        maskq[:, b, :], 1.0, LOWEST, ALU.add, ALU.max,
                                                        mx[:, n % 2, h:h + 1])
                    last.then_inc(masked, 1)
                    dve.wait_ge(masked, at(n + 1, BODY, turn))
                    dve.tensor_scalar(nmx[:, n % 2, :], mx[:, n % 2, :], -1.0, None, ALU.mult)\
                       .then_inc(maxed, 1)
                if n < SLOTS:
                    dve.wait_ge(expd, at(n + 1, BODY, turn))
                    if n >= 2:
                        dve.wait_ge(normd, at(n - 1, BODY, turn))
                    dve.reciprocal(rc[:, n % 2, :], rs[:, n % 2, :]).then_inc(recd, 1)
                if 1 <= n <= SLOTS:
                    dve.wait_ge(pT_hid, at(n, BODY, turn))
                    dve.tensor_tensor(pT_l[:], ps[:, 4, :], f(pT_h[:]), ALU.subtract).then_inc(pT_lod, 1)
                for t in tiles_of(n):
                    rope(t, turn)
                if n >= 2:
                    m = n - 2
                    dve.wait_ge(womm, at(m + 1, BODY, turn))
                    if m >= B:
                        dve.wait_ge(accd, at(m - B + 1, BODY, turn))
                    dve.tensor_tensor(xres[:, m % B, :], ps[:, 6, :], xres[:, m % B, :], ALU.add)\
                       .then_inc(accd, 1)
                if n < SLOTS:
                    dve.wait_ge(v_hid, at(n + 1, BODY, turn))
                    dve.tensor_tensor(v_l[:, n % 2, :], ps[:, 7, 0:P], f(v_h[:, n % 2, :]), ALU.subtract)\
                       .then_inc(v_lod, 1)

            for t in tiles_of(-1):
                rope(t, None)
            dve.wait_ge(in_mask, 16)
            for n in range(FIRST):
                slot(n)
            with dve.Fori(0, TURNS) as turn:
                for n in loop_slots:
                    slot(n, turn)
            for n in tail_slots:
                slot(n)

            dve.wait_ge(cw_hi, 1)
            dve.tensor_tensor(a_l[:], a_raw[:], f(a_h[:]), ALU.subtract).then_inc(cw_lo, 1)
            for b in range(B):
                dve.wait_ge(accd, SLOTS - B + b + 1)
                norm_stats(2, b)

            def norm_c(b):
                dve.wait_ge(powd, B + 2)
                if b >= 2:
                    dve.wait_ge(t3, b - 1)
                apply_norm(xn3[:, b % 2, :], 2, b).then_inc(xnd, 1)

            def split_c(b):
                cols = slice((b % 4) * S, (b % 4 + 1) * S)
                dve.wait_ge(t3_hi, b + 1)
                dve.tensor_tensor(xc_l[:, :, cols], ps[:, 4 + b % 2, :].rearrange("p (k t) -> p k t", k=KC),
                                  f(xc_h[:, :, cols]), ALU.subtract).then_inc(t3_lo, 1)
                dve.tensor_reduce(xs_f[:, b * S:(b + 1) * S],
                                  ps[:, 4 + b % 2, :].rearrange("p (k t) -> p t k", k=KC), AX.X, ALU.add)\
                   .then_inc(xsum, 1)

            def split_sum(hf):
                cols = slice(hf * HALF, (hf + 1) * HALF)
                dve.wait_ge(xs_hid, hf + 1)
                dve.tensor_tensor(xs_l[:, cols], xs_f[:, cols], f(xs_h[:, cols]), ALU.subtract)\
                   .then_inc(xs_lod, 1)
                dve.wait_ge(u_hid, hf + 1)
                dve.tensor_tensor(u_s[32:64, cols], ps[32:64, 6 + hf, :], f(u_s[32:64, cols]), ALU.subtract)\
                   .then_inc(u_lod, 1)

            norm_c(0)
            norm_c(1)
            for b in range(4):
                split_c(b)
                norm_c(b + 2)
            split_sum(0)
            for i, (hi, lo, raw) in enumerate(((g1_h, g1_l, g1_raw), (g3_h, g3_l, g3_raw))):
                dve.wait_ge(cw_hi, 2 + i)
                dve.tensor_tensor(lo[:], raw[:], f(hi[:]), ALU.subtract).then_inc(cw_lo, 1)
            for i, (stk, raw) in enumerate(((bg_s, bg_raw), (bu_s, bu_raw))):
                dve.wait_ge(cw_hi, 4 + i)
                dve.scalar_tensor_tensor(out=stk[64:STK, :], in0=raw[64:STK, :], scalar=0.5,
                                         in1=f(stk[64:STK, :]), op0=ALU.mult, op1=ALU.subtract)\
                   .then_inc(cw_lo, 1)
            for b in range(4, B):
                split_c(b)
                if b + 2 < B:
                    norm_c(b + 2)
            split_sum(1)

            def gate_up(hf, t, j):
                i = hf * FT * 4 + t * 4 + j
                rows = min(P, FQ - t * P)
                dst = gsum[0:rows, t, :] if j == 0 else gate[0:rows, i % 2, :]
                dve.wait_ge(sild, i + 1)
                if j == 0 and hf == 1:
                    dve.wait_ge(gs_lod, t + 1)
                if j and i >= 3:
                    dve.wait_ge(gsd, 3 * (i // 4) + max(j - 2, 0))
                dve.tensor_tensor(dst, ps[0:rows, 2 + i % 2, :], sil[0:rows, i % 2, :], ALU.mult)\
                   .then_inc(gated, 1)
                if i == FT * 4:
                    dve.wait_ge(l_lod, 1)
                dve.wait_ge(gated, i + 1)
                for r in range(RANK):
                    c = a2c[0:rows, t * 4 + j, r:r + 1]
                    if t == 0 and j == 0:
                        dve.tensor_scalar(lacc[:, r, :], dst, c, None, ALU.mult).then_inc(lod, 1)
                    else:
                        dve.wait_ge(lod, RANK * i + r - 1)
                        dve.scalar_tensor_tensor(out=lacc[0:rows, r, :], in0=dst, scalar=c,
                                                 in1=lacc[0:rows, r, :], op0=ALU.mult, op1=ALU.add)\
                           .then_inc(lod, 1)

            def split_gs(hf, t):
                rows = min(P, FQ - t * P)
                dve.wait_ge(gs_hid, hf * FT + t + 1)
                dve.tensor_tensor(gs_l[0:rows, t, :], gsum[0:rows, t, :], f(gs_h[0:rows, t, :]),
                                  ALU.subtract).then_inc(gs_lod, 1)

            def split_lora(hf):
                dve.wait_ge(l_hid, hf + 1)
                dve.tensor_tensor(lo_l[:], lacc[:], f(lo_h[:]), ALU.subtract).then_inc(l_lod, 1)

            def split_v(hf):
                dve.wait_ge(v3_hi, hf + 1)
                dve.tensor_tensor(v_s[32:64, :], ps[32:64, 6, :], f(v_s[32:64, :]), ALU.subtract)\
                   .then_inc(v3_lo, 1)

            def add_out(b):
                dve.wait_ge(down, b + 1)
                if b >= 2:
                    dve.wait_ge(stored[b % 2], 16 * (b // 2))
                dve.tensor_tensor(ost[:, b % 2, :], ps[:, (5, 7)[b % 2], :], xres[:, b, :], ALU.add)\
                   .then_inc(outd, 1)

            r = FQ - (FT - 1) * P
            dve.wait_ge(cw_hi, 6)
            dve.tensor_tensor(g2_l[:, 0:FT - 1, :], g2_raw[:, 0:FT - 1, :], f(g2_h[:, 0:FT - 1, :]),
                              ALU.subtract)
            dve.tensor_tensor(g2_l[0:r, FT - 1, :], g2_raw[0:r, FT - 1, :], f(g2_h[0:r, FT - 1, :]),
                              ALU.subtract).then_inc(cw_lo, 1)
            dve.wait_ge(cw_hi, 7)
            dve.scalar_tensor_tensor(out=bd_s[64:STK, :], in0=bd_raw[64:STK, :], scalar=0.5,
                                     in1=f(bd_s[64:STK, :]), op0=ALU.mult, op1=ALU.subtract)\
               .then_inc(cw_lo, 1)
            dve.wait_ge(cw_hi, 8)
            for hf in range(2):
                for t in range(FT):
                    for j in range(4):
                        if hf == 1 and t == 0 and j == 0:
                            split_gs(0, FT - 1)
                            split_lora(0)
                        if hf == 1 and t == 0 and j == 2:
                            split_v(0)
                            for b in range(4):
                                add_out(b)
                        if t >= 1 and j == 1:
                            split_gs(hf, t - 1)
                        gate_up(hf, t, j)
            split_gs(1, FT - 1)
            split_lora(1)
            split_v(1)
            for b in range(4, B):
                add_out(b)

        @block.gpsimd
        def _(pool):
            def chunk(c, turn=None):
                pool.wait_ge(chunk_hi, at(c + 1, CPT, turn))
                hi, lo = chunk_dst(c)
                pool.tensor_tensor(lo, stg[:, c % RING, :], f(hi), ALU.subtract).then_inc(chunk_lo, 1)

            pool.wait_ge(in_cst, 16)
            pool.wait_ge(vepd, B)
            pool.tensor_tensor(rstd[:, 0, :], vep[:, 0, :], minus_half, ALU.pow).then_inc(powd, 1)
            for b in range(B + 1):
                if b < B:
                    pool.wait_ge(gel, b + 1)
                    pool.tensor_tensor(xres[:, b, :], xres[:, b, :], yb[:, b % 2, :], ALU.add)\
                        .then_inc(x1d, 1)
                if b >= 1:
                    pool.wait_ge(vepd, B + b)
                    pool.tensor_tensor(rstd[:, 1, b - 1:b], vep[:, 1, b - 1:b], minus_half[:, 0:1], ALU.pow)\
                        .then_inc(powd, 1)
                if b < PRE // 2:
                    chunk(CH_A + 2 * b)
                    chunk(CH_A + 2 * b + 1)

            def add_rope(t, turn):
                half, e = t // TE, t % TE
                pool.wait_ge(rope_mul, at(t + 1, TPT, turn))
                pool.tensor_tensor(qr[:, half % 2, e, :], qr[:, half % 2, e, :], rot[:, t % 2, :], ALU.add)\
                    .then_inc(rope_add, 1)

            def split_q(n, turn):
                pool.wait_ge(q_hi, at(n + 1, BODY, turn))
                pool.tensor_tensor(qs_l[:, n % 2], qr[:, (n // 4) % 2, :, (n % 4) * P:(n % 4 + 1) * P],
                                   f(qs_h[:, n % 2]), ALU.subtract).then_inc(q_lo, 1)

            def slot(n, turn=None):
                if n < SLOTS:
                    for c in chunks_of(n):
                        chunk(c, turn)
                    pool.wait_ge(recd, at(n + 1, BODY, turn))
                    pool.tensor_tensor(pr[:, n % 2], pr[:, n % 2],
                                       rc[:, n % 2, :].rearrange("p (h a) -> p h a", a=1)
                                       .to_broadcast([P, HG, P]), ALU.mult).then_inc(normd, 1)
                if n + 1 < SLOTS:
                    split_q(n + 1, turn)
                for t in tiles_of(n):
                    add_rope(t, turn)

            for t in tiles_of(-1):
                add_rope(t, None)
                if t == TE - 1:
                    split_q(0, None)
            for n in range(FIRST):
                slot(n)
            with pool.Fori(0, TURNS) as turn:
                for n in loop_slots:
                    slot(n, turn)
            for n in tail_slots:
                slot(n)

            pool.wait_ge(vepd, 3 * B)
            pool.tensor_tensor(rstd[:, 2, :], vep[:, 2, :], minus_half, ALU.pow).then_inc(powd, 1)
            for i in range(2 * FT * 4):
                t, j = (i // 4) % FT, i % 4
                rows = min(P, FQ - t * P)
                if j:
                    pool.wait_ge(gated, i + 1)
                    if i > 1:
                        pool.wait_ge(gsd, 3 * (i // 4) + j - 1)
                    pool.tensor_tensor(gsum[0:rows, t, :], gsum[0:rows, t, :], gate[0:rows, i % 2, :],
                                       ALU.add).then_inc(gsd, 1)


def _rope_tables():
    inv = 1.0 / 10000.0 ** (np.arange(0, DK, 2, dtype=np.float32) / np.float32(DK))
    ang = np.arange(S, dtype=np.float32)[None, :] * inv.astype(np.float32)[:, None]
    share = np.float64(DK) ** -0.25
    c, s = np.cos(ang.astype(np.float32)) * share, np.sin(ang.astype(np.float32)) * share
    return np.concatenate([c, c]).astype(np.float32), np.concatenate([s, -s]).astype(np.float32)


def _stack(rows, at_row):
    st = np.zeros((STK, rows.shape[1]), rows.dtype)
    for g in range(3):
        st[32 * g + at_row:32 * g + at_row + RANK] = rows
    return st


def kernel(x, ctx_4096, mask_BxSxS2_ff0, L0_attn_w1, L0_attn_w2, L0_attn_b2, L0_attn_sparse_mask,
           L0_xattn_wq, L0_xattn_wk, L0_xattn_wv, L0_xattn_wo, L0_ffn_w1q, L0_ffn_a1, L0_ffn_b1,
           L0_ffn_w3q, L0_ffn_a3, L0_ffn_b3, L0_ffn_w2q, L0_ffn_a2, L0_ffn_b2):
    import concourse.bacc as _bacc
    from concourse.bass_utils import run_bass_kernel_spmd as _run

    a = np.asarray
    f32 = a(x).dtype
    stream = np.empty((NCH, P, 512), f32)
    w1, w2t = a(L0_attn_w1), a(L0_attn_w2).T
    ctxT = a(ctx_4096).reshape(TOK, D).T
    for k in range(KC):
        stream[2 * k] = w1[k * P:(k + 1) * P]
        stream[2 * k + 1] = w2t[k * P:(k + 1) * P]
        for hf in range(2):
            stream[CH_A + 2 * k + hf] = ctxT[k * P:(k + 1) * P, hf * HALF:(hf + 1) * HALF]

    def heads(w):
        w = a(w)
        return w.reshape(KC, P, -1, P).transpose(2, 1, 0, 3).reshape(-1, P, KC * P)
    body = stream[CH0:].reshape(KV, CH_G, P, 512)
    body[:, WK] = heads(L0_xattn_wk)
    body[:, WQ:WV] = heads(L0_xattn_wq).reshape(KV, HG, P, 512)
    body[:, WV] = heads(L0_xattn_wv)
    body[:, WO:] = a(L0_xattn_wo).reshape(KV, HG, P, D)

    cosT, sinT = _rope_tables()
    sel = np.zeros((P, RANK, STK), np.float32)
    for r in range(RANK):
        sel[:, r, r::32] = 1.0
    consts = np.concatenate([np.eye(P, dtype=np.float32), cosT, sinT, sel.reshape(P, -1),
                             np.full((P, 16), -0.5, np.float32)], axis=1)
    a_cols = np.ascontiguousarray((_stack(a(L0_ffn_a1), 0)[:, :]).T)
    a3 = _stack(a(L0_ffn_a3), RANK).T
    for g in range(3):
        a_cols[:, 32 * g + RANK:32 * g + 2 * RANK] = a3[:, 32 * g + RANK:32 * g + 2 * RANK]
    a2 = a(L0_ffn_a2).reshape(RANK, 4, FQ)
    a2_cols = np.zeros((P, FT, 4, RANK), f32)
    for t in range(FT):
        rows = min(P, FQ - t * P)
        a2_cols[:rows, t] = a2[:, :, t * P:t * P + rows].transpose(2, 1, 0)
    arrays = {
        "stream": stream, "x": a(x), "mask": a(mask_BxSxS2_ff0), "consts": consts,
        "spmask": a(L0_attn_sparse_mask), "b2": a(L0_attn_b2),
        "w1q": a(L0_ffn_w1q).T, "w3q": a(L0_ffn_w3q).T, "w2q": a(L0_ffn_w2q).T,
        "a_cols": a_cols, "bg_rows": _stack(a(L0_ffn_b1).T, 0), "bu_rows": _stack(a(L0_ffn_b3).T, RANK),
        "a2_cols": a2_cols.reshape(P, FT * 4, RANK), "b2_rows": _stack(a(L0_ffn_b2).T, 0),
    }
    nc = _bacc.Bacc("TRN2", target_bir_lowering=False, num_devices=1)
    given, args = {}, []
    for name, v in arrays.items():
        v = np.ascontiguousarray(v)
        given[f"in_{name}"] = v
        args.append(nc.dram_tensor(f"in_{name}", v.shape, mybir.dt.from_np(v.dtype), kind="ExternalInput").ap())
    args.append(nc.dram_tensor("out", (B, S, D), F32, kind="ExternalOutput").ap())
    decoder_block(nc, *args)
    r = _run(nc, [given], core_ids=[0])
    return r.results[0]["out"]
```

```python
from contextlib import ExitStack

import numpy as np

import concourse.bass as bass
from concourse import mybir

F32 = mybir.dt.float32
F32R = mybir.dt.float32r
ALU = mybir.AluOpType
ACT = mybir.ActivationFunctionType
AX = mybir.AxisListType

P = 128
B, S, D = 8, 128, 512
KC = D // P
TOK = B * S
HALF = TOK // 2
QH, KV, DK = 32, 8, 128
HG = QH // KV
FF = 1376
FQ = FF // 4
FT = (FQ + P - 1) // P
EPS = 1e-5
RANK = 2
STK = 96
LOWEST = -3.4e38

SLOTS = KV * B
TE = HG + 1
CH_A, CH_CTX = 8, 8
CH0 = CH_A + CH_CTX
CH_PAIR, CH_EVEN = 20, 11
NCH = CH0 + KV // 2 * CH_PAIR
WK, WQ = 0, 1
WV = WQ + HG
RING = 4
FIRST, BODY = 2, 16
TURNS = 3
SPLIT_AT = [[[0], [1], [2], [3], [4, 5], [6, 7], [8], [9, 10]],
            [[0], [1], [2], [3], [4], [5], [6], [7, 8]]]


def first_chunk(g):
    return CH0 + CH_PAIR * (g // 2) + CH_EVEN * (g % 2)


def place_of(c):
    p, i = (c - CH0) // CH_PAIR, (c - CH0) % CH_PAIR
    g, i = (2 * p, i) if i < CH_EVEN else (2 * p + 1, i - CH_EVEN)
    if i < WV:
        return g, ("k", 0) if i == WK else ("q", i - WQ)
    if g % 2 == 0 and i < WV + 2:
        return g, ("v", i - WV)
    return g, ("o", i - WV - 2 * (g % 2 == 0))


def tiles_of(n):
    if n == -1:
        return list(range(TE)) + [TE, TE + 1]
    half = {3: (n + 5) // 4, 0: (n + 4) // 4, 1: (n + 3) // 4, 2: (n + 2) // 4}[n % 4]
    if half >= 2 * KV:
        return []
    return [TE * half + e for e in {3: [0, 1], 0: [2], 1: [3], 2: [4]}[n % 4]]


def chunks_of(n):
    if n >= SLOTS - B:
        return []
    g = n // B + 1
    return [first_chunk(g) + i for i in SPLIT_AT[g % 2][n % B]]


def decoder_block(nc, stream, x, mask, consts, spmask, b2, w1q, w3q, w2q, a_cols, bg_rows, bu_rows,
                  a2_cols, b2_rows, out):
    with ExitStack() as ctx:
        def sem(name):
            return ctx.enter_context(nc.semaphore(name))

        def sb(scope, name, shape, dt=F32):
            return scope.enter_context(nc.sbuf_tensor(name, shape, dt))

        ps = ctx.enter_context(nc.psum_tensor("ps", [P, 8, 512], F32))
        xres = sb(ctx, "xres", [P, B, D])
        maskq = sb(ctx, "maskq", [P, B, S])
        cst = sb(ctx, "cst", [P, 4 * P + 2 * STK + B])
        stats = sb(ctx, "stats", [P, 2, 6])
        mv = sb(ctx, "mv", [P, 3, B, 2])
        vep = sb(ctx, "vep", [P, 3, B])
        rstd = sb(ctx, "rstd", [P, 3, B])
        mx = sb(ctx, "mx", [P, 2, HG])
        nmx = sb(ctx, "nmx", [P, 2, HG])
        rs = sb(ctx, "rs", [P, 2, HG])
        rc = sb(ctx, "rc", [P, 2, HG])
        ident = cst[:, 0:P]
        cosT, sinT = cst[:, P:2 * P], cst[:, 2 * P:3 * P]
        ones_raw = cst[0:2 * 32, 3 * P:4 * P]
        sel_raw = cst[:, 4 * P:4 * P + 2 * STK]
        minus_half = cst[:, 4 * P + 2 * STK:4 * P + 2 * STK + B]

        r1 = ExitStack()
        xT_h = sb(r1, "xT_h", [P, KC, TOK], F32R)
        xT_l = sb(r1, "xT_l", [P, KC, TOK], F32R)
        wq_h = sb(r1, "wq_h", [P, HG, KC, P], F32R)
        wq_l = sb(r1, "wq_l", [P, HG, KC, P], F32R)
        wk_h = sb(r1, "wk_h", [P, KC, P], F32R)
        wk_l = sb(r1, "wk_l", [P, KC, P], F32R)
        r2 = ExitStack()
        stg = sb(r2, "stg", [P, RING, 512])
        cT_h = sb(r2, "cT_h", [P, KC, TOK], F32R)
        cT_l = sb(r2, "cT_l", [P, KC, TOK], F32R)
        wv_h = sb(r2, "wv_h", [P, KC, 2, P], F32R)
        wv_l = sb(r2, "wv_l", [P, KC, 2, P], F32R)
        r3 = ExitStack()
        w1_h = sb(r3, "w1_h", [P, KC, D], F32R)
        w1_l = sb(r3, "w1_l", [P, KC, D], F32R)
        w2_h = sb(r3, "w2_h", [P, KC, D], F32R)
        w2_l = sb(r3, "w2_l", [P, KC, D], F32R)
        spm = sb(r3, "spm", [P, KC, D])
        atf = sb(r3, "atf", [P, KC, D])
        b2_raw = sb(r3, "b2_raw", [64, D])
        gap_a = sb(r3, "gap_a", [P, 6 * 256])
        at_h = sb(r3, "at_h", [P, KC, D], F32R)
        at_l = sb(r3, "at_l", [P, KC, D], F32R)
        xn = sb(r3, "xn", [P, 2, D])
        yb = sb(r3, "yb", [P, 2, D])
        b2_s = sb(r3, "b2_s", [64, D], F32R)
        ones = sb(r3, "ones", [64, P], F32R)
        r3.close()
        r3 = ExitStack()
        wo_h = sb(r3, "wo_h", [P, 2, HG, 512], F32R)
        wo_l = sb(r3, "wo_l", [P, 2, HG, 512], F32R)
        qr = sb(r3, "qr", [P, 2, TE, HALF])
        rot = sb(r3, "rot", [P, 2, HALF])
        qs_h = sb(r3, "qs_h", [P, TE, P], F32R)
        qs_l = sb(r3, "qs_l", [P, TE, P], F32R)
        pr = sb(r3, "pr", [P, 2, HG, P])
        pT_h = sb(r3, "pT_h", [P, HG * P], F32R)
        pT_l = sb(r3, "pT_l", [P, HG * P], F32R)
        o_h = sb(r3, "o_h", [P, HG * P], F32R)
        o_l = sb(r3, "o_l", [P, HG * P], F32R)
        ve_h = sb(r3, "ve_h", [P, 2, P], F32R)
        ve_l = sb(r3, "ve_l", [P, 2, P], F32R)
        vo_h = sb(r3, "vo_h", [P, B, P], F32R)
        vo_l = sb(r3, "vo_l", [P, B, P], F32R)
        r3.close()
        r2.close()
        r1.close()
        r1 = ExitStack()
        g1_h = sb(r1, "g1_h", [P, FF], F32R)
        g1_l = sb(r1, "g1_l", [P, FF], F32R)
        g3_h = sb(r1, "g3_h", [P, FF], F32R)
        g3_l = sb(r1, "g3_l", [P, FF], F32R)
        g1_raw = sb(r1, "g1_raw", [P, FF])
        g3_raw = sb(r1, "g3_raw", [P, FF])
        a_raw = sb(r1, "a_raw", [P, KC, STK])
        a_h = sb(r1, "a_h", [P, KC, STK], F32R)
        a_l = sb(r1, "a_l", [P, KC, STK], F32R)
        bg_s = sb(r1, "bg_s", [STK, FF], F32R)
        u_s = sb(r1, "u_s", [STK, TOK], F32R)
        a2c = sb(r1, "a2c", [P, FT * 4, RANK])
        gap_1 = sb(r1, "gap_1", [P, 52 * 256 - 7 * FF - 3 * KC * STK - TOK - FT * 4 * RANK])
        r2 = ExitStack()
        bg_raw = sb(r2, "bg_raw", [STK, FF])
        bu_raw = sb(r2, "bu_raw", [STK, FF])
        bu_s = sb(r2, "bu_s", [STK, FF], F32R)
        xs_f = sb(r2, "xs_f", [P, HALF])
        xs_h = sb(r2, "xs_h", [P, TOK], F32R)
        xs_l = sb(r2, "xs_l", [P, TOK], F32R)
        xn3 = sb(r2, "xn3", [P, 2, D])
        xc_h = sb(r2, "xc_h", [P, KC, HALF], F32R)
        xc_l = sb(r2, "xc_l", [P, KC, HALF], F32R)
        gap_2 = sb(r2, "gap_2", [P, 48 * 256 - 3 * FF - HALF - 2 * TOK - 2 * D - 2 * KC * HALF])
        r3 = ExitStack()
        g2_raw = sb(r3, "g2_raw", [P, FT, D])
        bd_raw = sb(r3, "bd_raw", [STK, D])
        gs_h = sb(r3, "gs_h", [P, FT, HALF], F32R)
        v_s = sb(r3, "v_s", [STK, HALF], F32R)
        g2_h = sb(r3, "g2_h", [P, FT, D], F32R)
        bd_s = sb(r3, "bd_s", [STK, D], F32R)
        gs_l = sb(r3, "gs_l", [P, FT, HALF], F32R)
        sel = sb(r3, "sel", [P, RANK, STK], F32R)
        gap_3 = sb(r3, "gap_3", [P, 2 * 256 - RANK * STK])
        gsum = sb(r3, "gsum", [P, FT, HALF])
        lacc = sb(r3, "lacc", [P, RANK + 1, HALF])
        sil = sb(r3, "sil", [P, 2, HALF])
        gate = sb(r3, "gate", [P, 2, HALF])
        prod = sb(r3, "prod", [P, HALF])
        g2_l = sb(r3, "g2_l", [P, FT, D], F32R)
        lo_h = sb(r3, "lo_h", [P, RANK, HALF], F32R)
        lo_l = sb(r3, "lo_l", [P, RANK, HALF], F32R)
        ost = sb(r3, "ost", [P, 4, D])
        r3.close()
        r2.close()
        r1.close()
        del gap_a, gap_1, gap_2, gap_3

        in_cst, in_b2, in_spm, in_mask = sem("in_cst"), sem("in_b2"), sem("in_spm"), sem("in_mask")
        in_x = [sem(f"in_x{b}") for b in range(B)]
        in_stg = [sem(f"in_stg{r}") for r in range(RING)]
        chunk_hi, chunk_lo, wlo = sem("chunk_hi"), sem("chunk_lo"), sem("wlo")
        agg, vepd, powd, xnd = sem("agg"), sem("vepd"), sem("powd"), sem("xnd")
        bns = sem("bns")
        wprod, attd, at_hid, at_lod = sem("wprod"), sem("attd"), sem("at_hid"), sem("at_lod")
        tr, tr_hi, tr_lo = sem("tr"), sem("tr_hi"), sem("tr_lo")
        ymm, gel, x1d, ones_d, b2_hi, b2_lo = (sem("ymm"), sem("gel"), sem("x1d"), sem("ones_d"),
                                               sem("b2_hi"), sem("b2_lo"))
        tile_mm, rope_mul, rope_add = sem("tile_mm"), sem("rope_mul"), sem("rope_add")
        q_hi, q_lo = sem("q_hi"), sem("q_lo")
        scored, masked, maxed, expd, recd, normd = (sem("scored"), sem("masked"), sem("maxed"),
                                                    sem("expd"), sem("recd"), sem("normd"))
        pT, pT_hid, pT_lod = sem("pT"), sem("pT_hid"), sem("pT_lod")
        vmm, v_hid, v_lod = sem("vmm"), sem("v_hid"), sem("v_lod")
        pv, o_hid, o_lod = sem("pv"), sem("o_hid"), sem("o_lod")
        womm, accd = sem("womm"), sem("accd")
        in_ff = [sem(f"in_ff{i}") for i in range(4)]
        a_hi, a_lo, g_hi, g_lo = sem("a_hi"), sem("a_lo"), sem("g_hi"), sem("g_lo")
        bs_hi, bs_lo, g2_hi, g2_lo = sem("bs_hi"), sem("bs_lo"), sem("g2_hi"), sem("g2_lo")
        bd_hi, bd_lo, seld = sem("bd_hi"), sem("bd_lo"), sem("seld")
        t3, t3_hi, t3_lo, xsum = sem("t3"), sem("t3_hi"), sem("t3_lo"), sem("xsum")
        xs_hid, xs_lod = sem("xs_hid"), sem("xs_lod")
        umm, u_hid, u_lod = sem("umm"), sem("u_hid"), sem("u_lod")
        gu, sild, gated, gsd, gs_hid, gs_lod = (sem("gu"), sem("sild"), sem("gated"), sem("gsd"),
                                                sem("gs_hid"), sem("gs_lod"))
        l_dve, prodd, l_pool, l_sum = sem("l_dve"), sem("prodd"), sem("l_pool"), sem("l_sum")
        l_hid, l_lod, vm, v3_hi, v3_lo = (sem("l_hid"), sem("l_lod"), sem("vm"), sem("v3_hi"),
                                          sem("v3_lo"))
        down, outd, stored = sem("down"), sem("outd"), [sem(f"stored{i}") for i in range(4)]

        def three(pe, dst, a_hi, a_lo, b_hi, b_lo, first, last):
            pe.matmul(dst, a_hi, b_hi, start=first, stop=False)
            pe.matmul(dst, a_hi, b_lo, start=False, stop=False)
            return pe.matmul(dst, a_lo, b_hi, start=False, stop=last)

        def f(ap):
            return ap.bitcast(F32)

        def at(value, per_turn, turn):
            return value if turn is None else turn * per_turn + value

        def chunk_dst(c):
            if c < CH_A:
                return (w2_h, w2_l)[0][:, c // 2] if c % 2 else w1_h[:, c // 2], \
                    w2_l[:, c // 2] if c % 2 else w1_l[:, c // 2]
            if c < CH0:
                k, hf = (c - CH_A) // 2, (c - CH_A) % 2
                cols = slice(hf * HALF, (hf + 1) * HALF)
                return cT_h[:, k, cols], cT_l[:, k, cols]
            g, (kind, i) = place_of(c)
            if kind == "v":
                return wv_h[:, :, i, :], wv_l[:, :, i, :]
            if kind == "o":
                return wo_h[:, g % 2, i, :], wo_l[:, g % 2, i, :]
            pair = (wk_h[:], wk_l[:]) if kind == "k" else (wq_h[:, i], wq_l[:, i])
            return tuple(p.rearrange("p k c -> p (k c)") for p in pair)

        def chunk_src(c):
            src = stg[:, c % RING, :]
            if c >= CH0 and place_of(c)[1][0] == "v":
                return src.rearrange("p (k c) -> p k c", k=KC)
            return src

        def values_of(n):
            b = n % B
            return (vo_h[:, b, :], vo_l[:, b, :]) if n // B % 2 else (ve_h[:, b % 2, :], ve_l[:, b % 2, :])

        def makes_values(n):
            return n < SLOTS and n // B % 2 == 0

        def value_count(n):
            return B * (n // (2 * B)) + (n % B + 1 if n // B % 2 == 0 else B)

        turns_a = [(1, 0), (1, 1)]
        for b in range(B + 2):
            turns_a += [(1, b + 2)] * (b + 2 < B) + [(2, b - 2)] * (b >= 2)
        place_a = {t: i for i, t in enumerate(turns_a)}

        early_tiles = {B - 1: [0], B: [1, 2], B + 1: [3, 4, 5, 6]}
        UPS = FT * 4
        TAIL = SLOTS - B + 2

        down_bank = [4, 5, 7, 4, 5, 7, 4, 0]

        def up_of(i):
            t = i % UPS // 4
            return i // UPS, t, i % 4, min(P, FQ - t * P)

        loop_slots = range(FIRST, FIRST + BODY)
        tail_slots = range(FIRST + BODY * TURNS, SLOTS + 2)
        TPT, CPT, VPT = TE * BODY // 4, CH_PAIR, B

        block = ctx.enter_context(nc.Block())

        @block.sync
        def _(sp):
            def load_chunk(c, turn=None, src=None):
                if c >= RING:
                    if c - RING < CH_A:
                        sp.wait_ge(wlo, c - RING + 1)
                    else:
                        sp.wait_ge(chunk_lo, at(c - RING - CH_A + 1, RING, turn))
                sp.dma_start(stg[:, c % RING, :], stream[c] if src is None else src)\
                  .then_inc(in_stg[c % RING], 16)

            for c in range(RING):
                load_chunk(c)
            sp.dma_start(cst[:], consts).then_inc(in_cst, 16)
            for b in range(2):
                sp.dma_start(xres[:, b, :], x[b]).then_inc(in_x[b], 16)
            for c in range(RING, CH_A):
                load_chunk(c)
            sp.dma_start(b2_raw[:], b2).then_inc(in_b2, 16)
            sp.dma_start(spm[:], spmask.rearrange("(m p) t -> p m t", p=P)).then_inc(in_spm, 16)
            for b in range(2, B):
                sp.dma_start(xres[:, b, :], x[b]).then_inc(in_x[b], 16)
            sp.dma_start(maskq[:], mask.rearrange("b q k -> q b k")).then_inc(in_mask, 16)
            for c in range(CH_A, 4 * RING):
                load_chunk(c)
            with sp.Fori(0, (NCH - 4 * RING) // RING) as turn:
                for r in range(RING):
                    place = sp.snap(turn * RING + (4 * RING + r))
                    load_chunk(4 * RING + r, turn, stream[bass.ds(place, 1)].rearrange("a p n -> (a p) n"))
            sp.wait_ge(tile_mm, TE * 2 * KV)
            sp.wait_ge(vmm, SLOTS // 2)
            sp.wait_ge(chunk_lo, NCH - CH_A)
            sp.dma_start(a_raw[:], a_cols.rearrange("(k p) c -> p k c", p=P)).then_inc(in_ff[0], 16)
            sp.dma_start(g1_raw[:], w1q).then_inc(in_ff[0], 16)
            sp.dma_start(g3_raw[:], w3q).then_inc(in_ff[0], 16)
            sp.dma_start(bg_raw[:], bg_rows).then_inc(in_ff[1], 16)
            sp.dma_start(bu_raw[:], bu_rows).then_inc(in_ff[1], 16)
            sp.dma_start(a2c[:], a2_cols).then_inc(in_ff[3], 16)
            sp.wait_ge(womm, SLOTS - B)
            sp.dma_start(g2_raw[:, 0:FT - 1, :], w2q[0:(FT - 1) * P].rearrange("(t p) n -> p t n", p=P))\
              .then_inc(in_ff[2], 16)
            sp.dma_start(g2_raw[0:FQ - (FT - 1) * P, FT - 1, :], w2q[(FT - 1) * P:FQ]).then_inc(in_ff[2], 16)
            sp.dma_start(bd_raw[:], b2_rows).then_inc(in_ff[2], 16)
            for b in range(B):
                sp.wait_ge(outd, b + 1)
                sp.dma_start(out[b], ost[:, b % 4, :]).then_inc(stored[b % 4], 16)
            for r in range(4):
                sp.wait_ge(stored[r], 16 * B // 4)

        @block.tensor
        def _(pe):
            for k in range(KC):
                pe.wait_ge(chunk_hi, 2 * k + 2)
                pe.wait_ge(wlo, 2 * k + 2)
                for m in range(KC):
                    cols = slice(m * P, (m + 1) * P)
                    mm = three(pe, ps[:, m, :], w1_h[:, k, cols], w1_l[:, k, cols],
                               w2_h[:, k, :], w2_l[:, k, :], k == 0, k == KC - 1)
                    if k == KC - 1:
                        mm.then_inc(wprod, 1)

            def transpose_a(norm, b):
                i = place_a[norm, b]
                pe.wait_ge(xnd, i + 1)
                if i >= 2:
                    pe.wait_ge(tr_lo, i - 1)
                for k in range(KC):
                    mm = pe.transpose(ps[:, 4 + i % 2, k * P:(k + 1) * P],
                                      xn[:, i % 2, k * P:(k + 1) * P], ident)
                mm.then_inc(tr, 1)

            def project(t, turn):
                half, e = t // TE, t % TE
                g = half // 2
                pe.wait_ge(chunk_lo, at(first_chunk(g) + e - CH_A + 1, CPT, turn))
                if t < 2 * TE:
                    pe.wait_ge(tr_lo, place_a[2, 4 * half + 3] + 1)
                if t >= 2:
                    pe.wait_ge(rope_mul, at(t - 1, TPT, turn))
                cols = slice((half % 2) * HALF, (half % 2 + 1) * HALF)
                for k in range(KC):
                    if e == 0:
                        mm = three(pe, ps[:, 2 + t % 2, :], wk_h[:, k, :], wk_l[:, k, :],
                                   cT_h[:, k, cols], cT_l[:, k, cols], k == 0, k == KC - 1)
                    else:
                        mm = three(pe, ps[:, 2 + t % 2, :], wq_h[:, e - 1, k, :], wq_l[:, e - 1, k, :],
                                   xT_h[:, k, cols], xT_l[:, k, cols], k == 0, k == KC - 1)
                mm.then_inc(tile_mm, 1)

            pe.wait_ge(in_cst, 16)
            transpose_a(1, 0)
            transpose_a(1, 1)
            for b in range(B + 2):
                if b < B:
                    pe.wait_ge(tr_lo, place_a[1, b] + 1)
                    if b >= 2:
                        pe.wait_ge(gel, b - 1)
                    cols = slice(b * S, (b + 1) * S)
                    for k in range(KC):
                        if b == 0:
                            pe.wait_ge(at_lod, k + 1)
                        three(pe, ps[:, 6 + b % 2, :], xT_h[:, k, cols], xT_l[:, k, cols],
                              at_h[:, k, :], at_l[:, k, :], k == 0, False)
                    if b == 0:
                        pe.wait_ge(b2_lo, 1)
                    pe.matmul(ps[:, 6 + b % 2, :], ones[:], b2_s[:], start=False, stop=True)\
                      .then_inc(ymm, 1)
                if b + 2 < B:
                    transpose_a(1, b + 2)
                if b >= 2:
                    transpose_a(2, b - 2)
                for t in early_tiles.get(b, []):
                    project(t, None)

            def slot(n, turn=None):
                b, g = n % B, n // B
                if n < SLOTS:
                    pe.wait_ge(q_lo, at(n + 1, BODY, turn))
                    if n >= 2:
                        pe.wait_ge(masked, at(n - 1, BODY, turn))
                    for h in range(HG):
                        mm = three(pe, ps[:, n % 2, h * P:(h + 1) * P],
                                   qs_h[:, 1 + h, :], qs_l[:, 1 + h, :],
                                   qs_h[:, 0, :], qs_l[:, 0, :], True, True)
                    mm.then_inc(scored, 1)
                for t in tiles_of(n):
                    project(t, turn)
                if 1 <= n <= SLOTS:
                    pe.wait_ge(normd, at(n, BODY, turn))
                    if n >= 2:
                        pe.wait_ge(pT_lod, at(n - 1, BODY, turn))
                    for h in range(HG):
                        mm = pe.transpose(ps[:, 4, h * P:(h + 1) * P], pr[:, (n - 1) % 2, h, :], ident)
                    mm.then_inc(pT, 1)
                if n >= 2:
                    m = n - 2
                    pe.wait_ge(o_lod, at(m + 1, BODY, turn))
                    pe.wait_ge(chunk_lo, at(first_chunk(m // B + 1) - CH_A, CPT, turn))
                    if m >= 1:
                        pe.wait_ge(accd, at(m, BODY, turn))
                    for h in range(HG):
                        cols = slice(h * P, (h + 1) * P)
                        mm = three(pe, ps[:, 6, :], o_h[:, cols], o_l[:, cols],
                                   wo_h[:, (m // B) % 2, h, :], wo_l[:, (m // B) % 2, h, :],
                                   h == 0, h == HG - 1)
                    mm.then_inc(womm, 1)
                if makes_values(n):
                    pe.wait_ge(chunk_lo, at(first_chunk(g) + WV + 2 - CH_A, CPT, turn))
                    if n >= 1:
                        pe.wait_ge(v_lod, at(value_count(n) - 1, VPT, turn))
                    cols = slice(b * S, (b + 1) * S)
                    for k in range(KC):
                        mm = three(pe, ps[:, 7, 0:2 * P], cT_h[:, k, cols], cT_l[:, k, cols],
                                   wv_h[:, k].rearrange("p g c -> p (g c)"),
                                   wv_l[:, k].rearrange("p g c -> p (g c)"), k == 0, k == KC - 1)
                    mm.then_inc(vmm, 1)
                if 1 <= n <= SLOTS:
                    m = n - 1
                    pe.wait_ge(pT_lod, at(m + 1, BODY, turn))
                    pe.wait_ge(v_lod, at(value_count(m), VPT, turn))
                    if m >= 1:
                        pe.wait_ge(o_lod, at(m, BODY, turn))
                    three(pe, ps[:, 5, :], *values_of(m), pT_h[:], pT_l[:], True, True).then_inc(pv, 1)

            def transpose_c(b):
                pe.wait_ge(xnd, len(turns_a) + b + 1)
                if b >= 1:
                    pe.wait_ge(xsum, b)
                for k in range(KC):
                    mm = pe.transpose(ps[:, 7, k * P:(k + 1) * P],
                                      xn3[:, b % 2, k * P:(k + 1) * P], ident)
                mm.then_inc(t3, 1)

            def lora_in(hf):
                pe.wait_ge(a_lo, 1)
                pe.wait_ge(t3_lo, 4 * hf + 4)
                for k in range(KC):
                    mm = three(pe, ps[0:STK, 3 + hf, :], a_h[:, k, :], a_l[:, k, :],
                               xc_h[:, k, :], xc_l[:, k, :], k == 0, k == KC - 1)
                mm.then_inc(umm, 1)

            def up(i):
                hf, t, j, rows = up_of(i)
                cols = slice(j * FQ + t * P, j * FQ + t * P + rows)
                toks = slice(hf * HALF, (hf + 1) * HALF)
                if i == 0:
                    pe.wait_ge(g_lo, 2)
                if i % UPS == 0:
                    pe.wait_ge(xs_lod, hf + 1)
                if i >= 2:
                    pe.wait_ge(gated, i - 1)
                for s, (w_h, w_l, rows_s) in enumerate(((g1_h, g1_l, bg_s), (g3_h, g3_l, bu_s))):
                    dst = ps[0:rows, 2 * s + i % 2, :]
                    three(pe, dst, w_h[:, cols], w_l[:, cols], xs_h[:, toks], xs_l[:, toks], True, False)
                    if i == 0:
                        pe.wait_ge(bs_lo, s + 1)
                    if i % UPS == 0:
                        pe.wait_ge(u_lod, hf + 1)
                    mm = pe.matmul(dst, rows_s[:, cols], u_s[:, toks], start=False, stop=True)
                mm.then_inc(gu, 1)

            def lora_out(hf):
                pe.wait_ge(seld, 1)
                pe.wait_ge(l_lod, hf + 1)
                if hf == 1:
                    pe.wait_ge(v3_lo, 1)
                for r in range(RANK):
                    pe.matmul(ps[0:STK, 6, :], sel[:, r, :], lo_h[:, r, :], start=(r == 0), stop=False)
                    mm = pe.matmul(ps[0:STK, 6, :], sel[:, r, :], lo_l[:, r, :], start=False,
                                   stop=(r == RANK - 1))
                mm.then_inc(vm, 1)

            def down_rows(b, t):
                if t == 0:
                    if b == 0:
                        pe.wait_ge(g2_lo, 1)
                    if 3 <= b < B - 1:
                        pe.wait_ge(outd, b - 2)
                    if b == B - 1:
                        pe.wait_ge(gated, 2 * UPS - 1)
                pe.wait_ge(gs_lod, FT * (b // 4) + t + 1)
                rows = min(P, FQ - t * P)
                cols = slice((b % 4) * S, (b % 4 + 1) * S)
                three(pe, ps[:, down_bank[b], :], gs_h[0:rows, t, cols], gs_l[0:rows, t, cols],
                      g2_h[0:rows, t, :], g2_l[0:rows, t, :], t == 0, False)

            def down_lora(b):
                pe.wait_ge(bd_lo, 1)
                pe.wait_ge(v3_lo, b // 4 + 1)
                cols = slice((b % 4) * S, (b % 4 + 1) * S)
                pe.matmul(ps[:, down_bank[b], :], v_s[:, cols], bd_s[:], start=False, stop=True)\
                  .then_inc(down, 1)

            for n in range(FIRST):
                slot(n)
            with pe.Fori(0, TURNS) as turn:
                for n in loop_slots:
                    slot(n, turn)
            for n in tail_slots:
                if n == SLOTS:
                    lora_in(0)
                if n >= TAIL + 2:
                    transpose_c(n - TAIL - 2)
                slot(n)
                if n == SLOTS:
                    up(0)
                    up(1)
            for i in range(2, UPS):
                up(i)
                if i == 3:
                    transpose_c(B - 2)
                if i == 5:
                    transpose_c(B - 1)
                if i == 7:
                    lora_in(1)
            for i in range(UPS, UPS + 2):
                up(i)
            lora_out(0)
            for b in range(4):
                for t in range(FT):
                    down_rows(b, t)
                down_lora(b)
            for i in range(UPS + 2, 2 * UPS):
                up(i)
            for t in range(FT):
                for b in range(4, B):
                    down_rows(b, t)
            lora_out(1)
            for b in range(4, B):
                down_lora(b)

        @block.scalar
        def _(act):
            def chunk(c, turn=None):
                act.wait_ge(in_stg[c % RING], at(16 * (c // RING + 1), 16 * CPT // RING, turn))
                if c >= CH0:
                    g, (kind, i) = place_of(c)
                    if kind in "kq" and g >= 1:
                        e = 0 if kind == "k" else 1 + i
                        act.wait_ge(tile_mm, at(TE * (2 * g - 1) + e + 1, TPT, turn))
                    elif kind == "v" and g >= 2:
                        act.wait_ge(vmm, at(B * (g // 2), VPT, turn))
                    elif kind == "o" and g >= 2:
                        act.wait_ge(womm, at(B * (g - 1), BODY, turn))
                    elif kind == "o":
                        act.wait_ge(wprod, KC)
                act.copy(chunk_dst(c)[0], chunk_src(c)).then_inc(chunk_hi, 1)

            for c in range(CH_A):
                chunk(c)
            act.wait_ge(in_cst, 16)
            act.copy(ones[:], ones_raw).then_inc(ones_d, 1)
            act.wait_ge(in_b2, 16)
            act.wait_ge(ones_d, 1)
            act.copy(b2_s[:], b2_raw[:]).then_inc(b2_hi, 1)
            for m in range(KC):
                act.wait_ge(attd, m + 1)
                act.copy(at_h[:, m, :], atf[:, m, :]).then_inc(at_hid, 1)

            def split_a(norm, b):
                i = place_a[norm, b]
                act.wait_ge(tr, i + 1)
                act.copy(xT_h[:, :, b * S:(b + 1) * S],
                         ps[:, 4 + i % 2, :].rearrange("p (k t) -> p k t", k=KC)).then_inc(tr_hi, 1)

            split_a(1, 0)
            split_a(1, 1)
            for c in range(CH_A, CH_A + 4):
                chunk(c)
            for b in range(B + 2):
                if b < B:
                    act.wait_ge(ymm, b + 1)
                    if b >= 2:
                        act.wait_ge(x1d, b - 1)
                    act.activation(yb[:, b % 2, :], ps[:, 6 + b % 2, :], ACT.Gelu).then_inc(gel, 1)
                if b + 2 < B:
                    split_a(1, b + 2)
                if b >= 2:
                    split_a(2, b - 2)
                for c in range(CH_A + 4 + 2 * b, min(CH_A + 6 + 2 * b, CH0 + CH_EVEN)):
                    chunk(c)

            def split_q(n, turn):
                act.wait_ge(rope_add, at(TE * (n // 4) + TE, TPT, turn))
                if n >= 1:
                    act.wait_ge(scored, at(n, BODY, turn))
                act.copy(qs_h[:], qr[:, (n // 4) % 2, :, (n % 4) * P:(n % 4 + 1) * P]).then_inc(q_hi, 1)

            def slot(n, turn=None):
                if n >= 2:
                    m = n - 2
                    act.wait_ge(pv, at(m + 1, BODY, turn))
                    if m >= 1:
                        act.wait_ge(womm, at(m, BODY, turn))
                    act.copy(o_h[:], ps[:, 5, :]).then_inc(o_hid, 1)
                if n + 1 < SLOTS:
                    split_q(n + 1, turn)
                if n < SLOTS:
                    act.wait_ge(maxed, at(n + 1, BODY, turn))
                    for h in range(HG):
                        last = act.activation(pr[:, n % 2, h, :], pr[:, n % 2, h, :], ACT.Exp,
                                              bias=nmx[:, n % 2, h:h + 1], scale=1.0,
                                              accum_out=rs[:, n % 2, h:h + 1])
                    last.then_inc(expd, 1)
                if 1 <= n <= SLOTS:
                    act.wait_ge(pT, at(n, BODY, turn))
                    if n >= 2:
                        act.wait_ge(pv, at(n - 1, BODY, turn))
                    act.copy(pT_h[:], ps[:, 4, :]).then_inc(pT_hid, 1)
                for c in chunks_of(n):
                    chunk(c, turn)
                if makes_values(n):
                    act.wait_ge(vmm, at(value_count(n), VPT, turn))
                    if n >= 2:
                        act.wait_ge(pv, at(n - 1, BODY, turn))
                    act.copy(values_of(n)[0], ps[:, 7, 0:P])
                    act.copy(values_of(n + B)[0], ps[:, 7, P:2 * P]).then_inc(v_hid, 1)

            def weights_hi(n):
                if n == TAIL + 1:
                    act.wait_ge(in_ff[0], 3 * 16)
                    act.copy(a_h[:], a_raw[:]).then_inc(a_hi, 1)
                    act.copy(g1_h[:], g1_raw[:]).then_inc(g_hi, 1)
                if n == TAIL + 2:
                    act.copy(g3_h[:], g3_raw[:]).then_inc(g_hi, 1)
                    act.wait_ge(in_ff[1], 2 * 16)
                    act.mul(bg_s[:], bg_raw[:], 0.5).then_inc(bs_hi, 1)
                if n == TAIL + 3:
                    act.mul(bu_s[:], bu_raw[:], 0.5).then_inc(bs_hi, 1)

            def split_c(b):
                act.wait_ge(t3, b + 1)
                if b >= 4:
                    act.wait_ge(umm, 1)
                act.copy(xc_h[:, :, (b % 4) * S:(b % 4 + 1) * S],
                         ps[:, 7, :].rearrange("p (k t) -> p k t", k=KC)).then_inc(t3_hi, 1)

            def split_sum(hf):
                cols = slice(hf * HALF, (hf + 1) * HALF)
                act.wait_ge(xsum, 4 * hf + 4)
                act.copy(xs_h[:, cols], xs_f[:]).then_inc(xs_hid, 1)
                act.wait_ge(umm, hf + 1)
                act.copy(u_s[:, cols], ps[0:STK, 3 + hf, :]).then_inc(u_hid, 1)

            def silu(i):
                hf, t, j, rows = up_of(i)
                act.wait_ge(gu, i + 1)
                if i >= 2:
                    act.wait_ge(gated, i - 1)
                act.activation(sil[0:rows, i % 2, :], ps[0:rows, i % 2, :], ACT.Silu).then_inc(sild, 1)

            def weigh(i):
                hf, t, j, rows = up_of(i)
                act.wait_ge(gated, i + 1)
                if i % UPS == 1:
                    if hf == 1:
                        act.wait_ge(l_sum, 1)
                    dst = lacc[0:rows, RANK, :]
                else:
                    if i >= 5:
                        act.wait_ge(l_pool, (i - 3) // 2 - i // UPS)
                    dst = prod[0:rows, :]
                act.activation(dst, gate[0:rows, i % 2, :], ACT.Copy, scale=a2c[0:rows, t * 4 + j, 1:2])\
                   .then_inc(prodd, 1)

            def split_gs(hf, t):
                rows = min(P, FQ - t * P)
                act.wait_ge(gsd, (hf * FT + t + 1) * 3)
                if hf == 1:
                    act.wait_ge(down, 4)
                elif t == 0:
                    act.wait_ge(womm, SLOTS)
                act.copy(gs_h[0:rows, t, :], gsum[0:rows, t, :]).then_inc(gs_hid, 1)

            def split_lora(hf):
                act.wait_ge(l_sum, hf + 1)
                if hf == 1:
                    act.wait_ge(vm, 1)
                act.copy(lo_h[:], lacc[:, 0:RANK, :]).then_inc(l_hid, 1)

            def split_v(hf):
                act.wait_ge(vm, hf + 1)
                if hf == 1:
                    act.wait_ge(down, 4)
                act.copy(v_s[:], ps[0:STK, 6, :]).then_inc(v3_hi, 1)

            split_q(0, None)
            for n in range(FIRST):
                slot(n)
            with act.Fori(0, TURNS) as turn:
                for n in loop_slots:
                    slot(n, turn)
            for n in tail_slots:
                if n == SLOTS:
                    split_sum(0)
                slot(n)
                weights_hi(n)
                if TAIL + 2 <= n <= SLOTS:
                    split_c(n - TAIL - 2)
            act.wait_ge(in_ff[3], 16)
            for i in range(2 * UPS):
                silu(i)
                if i % 2:
                    weigh(i)
                if i == 1:
                    split_c(B - 3)
                if i == 3:
                    split_c(B - 2)
                if i == 5:
                    split_c(B - 1)
                    act.wait_ge(womm, SLOTS)
                    act.wait_ge(in_ff[2], 3 * 16)
                    act.copy(g2_h[:, 0:FT - 1, :], g2_raw[:, 0:FT - 1, :])
                    act.copy(g2_h[0:FQ - (FT - 1) * P, FT - 1, :], g2_raw[0:FQ - (FT - 1) * P, FT - 1, :])\
                       .then_inc(g2_hi, 1)
                if i == 7:
                    split_sum(1)
                    act.mul(bd_s[:], bd_raw[:], 0.5).then_inc(bd_hi, 1)
                    act.copy(sel[:], sel_raw.rearrange("p (r c) -> p r c", r=RANK)).then_inc(seld, 1)
                if i % 4 == 0 and i:
                    split_gs((i // 4 - 1) // FT, (i // 4 - 1) % FT)
                if i == UPS:
                    split_lora(0)
                if i == UPS + 1:
                    split_v(0)
            split_gs(1, FT - 1)
            split_lora(1)
            split_v(1)

        @block.vector
        def _(dve):
            def norm_stats(norm, b):
                i = norm * B + b
                if i >= 2:
                    dve.wait_ge(agg, i - 1)
                dve.bn_stats(stats[:, i % 2, :], xres[:, b, :]).then_inc(bns, 1)
                dve.wait_ge(bns, i + 1)
                dve.bn_aggr(mv[:, norm, b, :], stats[:, i % 2, :]).then_inc(agg, 1)
                dve.wait_ge(agg, i + 1)
                dve.tensor_scalar(vep[:, norm, b:b + 1], mv[:, norm, b, 1:2], EPS, None, ALU.add)\
                   .then_inc(vepd, 1)

            def apply_norm(dst, norm, b):
                return dve.tensor_scalar(dst, xres[:, b, :], mv[:, norm, b, 0:1],
                                         rstd[:, norm, b:b + 1], ALU.subtract, ALU.mult)

            def norm_a(norm, b):
                i = place_a[norm, b]
                dve.wait_ge(powd, (1 if b < 2 else 2) if norm == 1 else b + 3)
                if i >= 2:
                    dve.wait_ge(tr, i - 1)
                apply_norm(xn[:, i % 2, :], norm - 1, b).then_inc(xnd, 1)

            def split_a(norm, b):
                i = place_a[norm, b]
                cols = slice(b * S, (b + 1) * S)
                dve.wait_ge(tr_hi, i + 1)
                dve.tensor_tensor(xT_l[:, :, cols], ps[:, 4 + i % 2, :].rearrange("p (k t) -> p k t", k=KC),
                                  f(xT_h[:, :, cols]), ALU.subtract).then_inc(tr_lo, 1)

            for c in range(CH_A):
                dve.wait_ge(chunk_hi, c + 1)
                hi, lo = chunk_dst(c)
                dve.tensor_tensor(lo, stg[:, c % RING, :], f(hi), ALU.subtract).then_inc(wlo, 1)
                if c in (3, 4):
                    dve.wait_ge(in_x[c - 3], 16)
                    norm_stats(0, c - 3)
            norm_a(1, 0)
            norm_a(1, 1)
            dve.wait_ge(b2_hi, 1)
            dve.tensor_tensor(b2_s[32:64, :], b2_raw[32:64, :], f(b2_s[32:64, :]), ALU.subtract)\
               .then_inc(b2_lo, 1)
            dve.wait_ge(in_spm, 16)
            for m in range(KC):
                dve.wait_ge(wprod, m + 1)
                dve.tensor_tensor(atf[:, m, :], ps[:, m, :], spm[:, m, :], ALU.mult).then_inc(attd, 1)
            split_a(1, 0)
            for m in range(KC):
                dve.wait_ge(at_hid, m + 1)
                dve.tensor_tensor(at_l[:, m, :], atf[:, m, :], f(at_h[:, m, :]), ALU.subtract)\
                   .then_inc(at_lod, 1)
            split_a(1, 1)
            for b in range(2, B):
                dve.wait_ge(in_x[b], 16)
                norm_stats(0, b)
            def rope(t, turn):
                half, e = t // TE, t % TE
                dve.wait_ge(tile_mm, at(t + 1, TPT, turn))
                if half >= 2:
                    dve.wait_ge(q_lo, at(4 * half - 4, BODY, turn))
                if t >= 2:
                    dve.wait_ge(rope_add, at(t - 1, TPT, turn))
                src = ps[:, 2 + t % 2, :].rearrange("p (b s) -> p b s", b=4)
                dst = rot[:, t % 2, :].rearrange("p (b s) -> p b s", b=4)
                h = DK // 2

                def table(lo, hi, tab):
                    return tab[lo:hi, :].rearrange("p (a s) -> p a s", a=1).to_broadcast([hi - lo, 4, S])
                dve.tensor_tensor(qr[:, half % 2, e, :].rearrange("p (b s) -> p b s", b=4), src,
                                  table(0, DK, cosT), ALU.mult)
                dve.tensor_tensor(dst[0:h], src[h:DK], table(h, DK, sinT), ALU.mult)
                dve.tensor_tensor(dst[h:DK], src[0:h], table(0, h, sinT), ALU.mult).then_inc(rope_mul, 1)

            for b in range(B + 2):
                if b + 2 < B:
                    norm_a(1, b + 2)
                    split_a(1, b + 2)
                if 1 <= b <= B:
                    dve.wait_ge(x1d, b)
                    norm_stats(1, b - 1)
                if b >= 2:
                    norm_a(2, b - 2)
                    split_a(2, b - 2)
                for t in early_tiles.get(b, []):
                    rope(t, None)

            def slot(n, turn=None):
                b = n % B
                if n >= 2:
                    dve.wait_ge(o_hid, at(n - 1, BODY, turn))
                if n < SLOTS:
                    if n >= 2:
                        dve.wait_ge(pT, at(n - 1, BODY, turn))
                    dve.wait_ge(scored, at(n + 1, BODY, turn))
                if n >= 2:
                    dve.tensor_tensor(o_l[:], ps[:, 5, :], f(o_h[:]), ALU.subtract).then_inc(o_lod, 1)
                if n < SLOTS:
                    for h in range(HG):
                        last = dve.tensor_tensor_reduce(pr[:, n % 2, h, :], ps[:, n % 2, h * P:(h + 1) * P],
                                                        maskq[:, b, :], 1.0, LOWEST, ALU.add, ALU.max,
                                                        mx[:, n % 2, h:h + 1])
                    last.then_inc(masked, 1)
                    dve.wait_ge(masked, at(n + 1, BODY, turn))
                    dve.tensor_scalar(nmx[:, n % 2, :], mx[:, n % 2, :], -1.0, None, ALU.mult)\
                       .then_inc(maxed, 1)
                if n < SLOTS:
                    dve.wait_ge(expd, at(n + 1, BODY, turn))
                    if n >= 2:
                        dve.wait_ge(normd, at(n - 1, BODY, turn))
                    dve.reciprocal(rc[:, n % 2, :], rs[:, n % 2, :]).then_inc(recd, 1)
                if 1 <= n <= SLOTS:
                    dve.wait_ge(pT_hid, at(n, BODY, turn))
                    dve.tensor_tensor(pT_l[:], ps[:, 4, :], f(pT_h[:]), ALU.subtract).then_inc(pT_lod, 1)
                for t in tiles_of(n):
                    rope(t, turn)
                if n >= 2:
                    m = n - 2
                    dve.wait_ge(womm, at(m + 1, BODY, turn))
                    if m >= B:
                        dve.wait_ge(accd, at(m - B + 1, BODY, turn))
                    dve.tensor_tensor(xres[:, m % B, :], ps[:, 6, :], xres[:, m % B, :], ALU.add)\
                       .then_inc(accd, 1)
                    if n >= TAIL:
                        dve.wait_ge(accd, n - 1)
                        norm_stats(2, n - TAIL)
                if makes_values(n):
                    dve.wait_ge(v_hid, at(value_count(n), VPT, turn))
                    for i in range(2):
                        hi, lo = values_of(n + B * i)
                        last = dve.tensor_tensor(lo, ps[:, 7, i * P:(i + 1) * P], f(hi), ALU.subtract)
                    last.then_inc(v_lod, 1)

            def norm_c(b):
                dve.wait_ge(powd, B + 3 + b)
                if b >= 2:
                    dve.wait_ge(t3, b - 1)
                elif b == 0:
                    dve.wait_ge(tile_mm, TE * 2 * KV)
                apply_norm(xn3[:, b % 2, :], 2, b).then_inc(xnd, 1)

            def split_c(b):
                cols = slice((b % 4) * S, (b % 4 + 1) * S)
                dve.wait_ge(t3_hi, b + 1)
                dve.tensor_tensor(xc_l[:, :, cols], ps[:, 7, :].rearrange("p (k t) -> p k t", k=KC),
                                  f(xc_h[:, :, cols]), ALU.subtract).then_inc(t3_lo, 1)
                dve.tensor_reduce(xs_f[:, cols], ps[:, 7, :].rearrange("p (k t) -> p t k", k=KC),
                                  AX.X, ALU.add).then_inc(xsum, 1)

            def split_sum(hf):
                cols = slice(hf * HALF, (hf + 1) * HALF)
                dve.wait_ge(xs_hid, hf + 1)
                dve.tensor_tensor(xs_l[:, cols], xs_f[:], f(xs_h[:, cols]), ALU.subtract)\
                   .then_inc(xs_lod, 1)
                dve.wait_ge(u_hid, hf + 1)
                dve.tensor_tensor(u_s[32:64, cols], ps[32:64, 3 + hf, :], f(u_s[32:64, cols]), ALU.subtract)\
                   .then_inc(u_lod, 1)

            def stack_lo(stk, raw, src, count, done):
                dve.wait_ge(src, count)
                dve.scalar_tensor_tensor(out=stk[64:STK, :], in0=raw[64:STK, :], scalar=0.5,
                                         in1=f(stk[64:STK, :]), op0=ALU.mult, op1=ALU.subtract)\
                   .then_inc(done, 1)

            def gate_up(i):
                hf, t, j, rows = up_of(i)
                dst = gsum[0:rows, t, :] if j == 0 else gate[0:rows, i % 2, :]
                dve.wait_ge(sild, i + 1)
                if j == 0 and hf == 1:
                    dve.wait_ge(gs_lod, t + 1)
                if j and i >= 3:
                    dve.wait_ge(gsd, 3 * (i // 4) + max(j - 2, 0))
                    if j % 2:
                        dve.wait_ge(prodd, i // 2)
                dve.tensor_tensor(dst, ps[0:rows, 2 + i % 2, :], sil[0:rows, i % 2, :], ALU.mult)\
                   .then_inc(gated, 1)
                if i == UPS:
                    dve.wait_ge(l_lod, 1)
                dve.wait_ge(gated, i + 1)
                for r in range(RANK):
                    if r == 1 and i % 2:
                        continue
                    c = a2c[0:rows, t * 4 + j, r:r + 1]
                    if i % UPS == 0:
                        dve.tensor_scalar(lacc[:, r, :], dst, c, None, ALU.mult).then_inc(l_dve, 1)
                    else:
                        dve.wait_ge(l_dve, 3 * (i // 2) + (0 if r == 0 else -1) + (r == 0 and i % 2))
                        dve.scalar_tensor_tensor(out=lacc[0:rows, r, :], in0=dst, scalar=c,
                                                 in1=lacc[0:rows, r, :], op0=ALU.mult, op1=ALU.add)\
                           .then_inc(l_dve, 1)

            def split_gs(hf, t):
                rows = min(P, FQ - t * P)
                dve.wait_ge(gs_hid, hf * FT + t + 1)
                dve.tensor_tensor(gs_l[0:rows, t, :], gsum[0:rows, t, :], f(gs_h[0:rows, t, :]),
                                  ALU.subtract).then_inc(gs_lod, 1)

            def split_lora(hf):
                dve.wait_ge(l_dve, (hf + 1) * UPS * 3 // 2)
                dve.wait_ge(l_pool, (hf + 1) * (UPS // 2 - 1))
                dve.tensor_tensor(lacc[:, 1, :], lacc[:, 1, :], lacc[:, RANK, :], ALU.add)\
                   .then_inc(l_sum, 1)
                dve.wait_ge(l_hid, hf + 1)
                dve.tensor_tensor(lo_l[:], lacc[:, 0:RANK, :], f(lo_h[:]), ALU.subtract)\
                   .then_inc(l_lod, 1)

            def split_v(hf):
                dve.wait_ge(v3_hi, hf + 1)
                dve.tensor_tensor(v_s[32:64, :], ps[32:64, 6, :], f(v_s[32:64, :]), ALU.subtract)\
                   .then_inc(v3_lo, 1)

            def add_out(b):
                dve.wait_ge(down, b + 1)
                if b >= 4:
                    dve.wait_ge(stored[b % 4], 16)
                dve.tensor_tensor(ost[:, b % 4, :], ps[:, down_bank[b], :], xres[:, b, :], ALU.add)\
                   .then_inc(outd, 1)

            dve.wait_ge(in_mask, 16)
            for n in range(FIRST):
                slot(n)
            with dve.Fori(0, TURNS) as turn:
                for n in loop_slots:
                    slot(n, turn)
            for n in tail_slots:
                if n == SLOTS:
                    split_sum(0)
                slot(n)
                if n >= TAIL + 1:
                    norm_c(n - TAIL - 1)
                if n == TAIL + 1:
                    dve.wait_ge(a_hi, 1)
                    dve.tensor_tensor(a_l[:], a_raw[:], f(a_h[:]), ALU.subtract).then_inc(a_lo, 1)
                if n == TAIL + 3:
                    stack_lo(bg_s, bg_raw, bs_hi, 1, bs_lo)
                if n == TAIL + 4:
                    stack_lo(bu_s, bu_raw, bs_hi, 2, bs_lo)
                if TAIL + 2 <= n <= SLOTS:
                    split_c(n - TAIL - 2)
            dve.wait_ge(in_ff[3], 16)
            for i in range(2 * UPS):
                if i % 4 == 1 and i > 1:
                    split_gs((i // 4 - 1) // FT, (i // 4 - 1) % FT)
                if i == UPS:
                    split_lora(0)
                gate_up(i)
                if i == 1:
                    norm_c(B - 1)
                    split_c(B - 3)
                if i == 3:
                    split_c(B - 2)
                if i == 5:
                    split_c(B - 1)
                if i == 7:
                    split_sum(1)
                    stack_lo(bd_s, bd_raw, bd_hi, 1, bd_lo)
                if i == UPS + 1:
                    split_v(0)
                    for b in range(4):
                        add_out(b)
            split_gs(1, FT - 1)
            split_lora(1)
            split_v(1)
            for b in range(4, B):
                add_out(b)

        @block.gpsimd
        def _(pool):
            def chunk(c, turn=None):
                pool.wait_ge(chunk_hi, at(c + 1, CPT, turn))
                hi, lo = chunk_dst(c)
                pool.tensor_tensor(lo, chunk_src(c), f(hi), ALU.subtract).then_inc(chunk_lo, 1)

            pool.wait_ge(in_cst, 16)
            for lo, hi in ((0, 2), (2, B)):
                pool.wait_ge(vepd, hi)
                pool.tensor_tensor(rstd[:, 0, lo:hi], vep[:, 0, lo:hi], minus_half[:, lo:hi], ALU.pow)\
                    .then_inc(powd, 1)
                if lo == 0:
                    for c in range(CH_A, CH_A + 4):
                        chunk(c)
            for b in range(B + 2):
                if b < B:
                    pool.wait_ge(gel, b + 1)
                    pool.tensor_tensor(xres[:, b, :], xres[:, b, :], yb[:, b % 2, :], ALU.add)\
                        .then_inc(x1d, 1)
                if 1 <= b <= B:
                    pool.wait_ge(vepd, B + b)
                    pool.tensor_tensor(rstd[:, 1, b - 1:b], vep[:, 1, b - 1:b], minus_half[:, 0:1], ALU.pow)\
                        .then_inc(powd, 1)
                for c in range(CH_A + 4 + 2 * b, min(CH_A + 6 + 2 * b, CH0 + CH_EVEN)):
                    chunk(c)

            def add_rope(t, turn):
                half, e = t // TE, t % TE
                pool.wait_ge(rope_mul, at(t + 1, TPT, turn))
                pool.tensor_tensor(qr[:, half % 2, e, :], qr[:, half % 2, e, :], rot[:, t % 2, :], ALU.add)\
                    .then_inc(rope_add, 1)

            def split_q(n, turn):
                pool.wait_ge(q_hi, at(n + 1, BODY, turn))
                pool.tensor_tensor(qs_l[:], qr[:, (n // 4) % 2, :, (n % 4) * P:(n % 4 + 1) * P],
                                   f(qs_h[:]), ALU.subtract).then_inc(q_lo, 1)

            def slot(n, turn=None):
                if n + 1 < SLOTS:
                    split_q(n + 1, turn)
                if n < SLOTS:
                    pool.wait_ge(recd, at(n + 1, BODY, turn))
                    pool.tensor_tensor(pr[:, n % 2], pr[:, n % 2],
                                       rc[:, n % 2, :].rearrange("p (h a) -> p h a", a=1)
                                       .to_broadcast([P, HG, P]), ALU.mult).then_inc(normd, 1)
                for c in chunks_of(n):
                    chunk(c, turn)
                for t in tiles_of(n):
                    add_rope(t, turn)

            for t in tiles_of(-1):
                add_rope(t, None)
                if t == TE - 1:
                    split_q(0, None)
            for n in range(FIRST):
                slot(n)
            with pool.Fori(0, TURNS) as turn:
                for n in loop_slots:
                    slot(n, turn)
            def inverse_c(b):
                pool.wait_ge(vepd, 2 * B + b + 1)
                pool.tensor_tensor(rstd[:, 2, b:b + 1], vep[:, 2, b:b + 1], minus_half[:, 0:1], ALU.pow)\
                    .then_inc(powd, 1)

            for n in tail_slots:
                slot(n)
                if n in (TAIL + 2, TAIL + 3):
                    i = n - TAIL - 2
                    hi, lo, raw = ((g1_h, g1_l, g1_raw), (g3_h, g3_l, g3_raw))[i]
                    pool.wait_ge(g_hi, i + 1)
                    pool.tensor_tensor(lo[:], raw[:], f(hi[:]), ALU.subtract).then_inc(g_lo, 1)
                if n >= TAIL:
                    inverse_c(n - TAIL)
            for i in range(2 * UPS):
                hf, t, j, rows = up_of(i)
                if j:
                    pool.wait_ge(gated, i + 1)
                    if i > 1:
                        pool.wait_ge(gsd, 3 * (i // 4) + j - 1)
                    pool.tensor_tensor(gsum[0:rows, t, :], gsum[0:rows, t, :], gate[0:rows, i % 2, :],
                                       ALU.add).then_inc(gsd, 1)
                if i % 2 and i % UPS != 1:
                    pool.wait_ge(prodd, (i + 1) // 2)
                    if i > 3:
                        pool.wait_ge(l_pool, (i - 1) // 2 - 1 - i // UPS)
                    pool.tensor_tensor(lacc[0:rows, RANK, :], lacc[0:rows, RANK, :], prod[0:rows, :],
                                       ALU.add).then_inc(l_pool, 1)
                if i == 4:
                    r = FQ - (FT - 1) * P
                    pool.wait_ge(g2_hi, 1)
                    pool.tensor_tensor(g2_l[:, 0:FT - 1, :], g2_raw[:, 0:FT - 1, :],
                                       f(g2_h[:, 0:FT - 1, :]), ALU.subtract)
                    pool.tensor_tensor(g2_l[0:r, FT - 1, :], g2_raw[0:r, FT - 1, :],
                                       f(g2_h[0:r, FT - 1, :]), ALU.subtract).then_inc(g2_lo, 1)


def _rope_tables():
    inv = 1.0 / 10000.0 ** (np.arange(0, DK, 2, dtype=np.float32) / np.float32(DK))
    ang = np.arange(S, dtype=np.float32)[None, :] * inv.astype(np.float32)[:, None]
    share = np.float64(DK) ** -0.25
    c, s = np.cos(ang.astype(np.float32)) * share, np.sin(ang.astype(np.float32)) * share
    return np.concatenate([c, c]).astype(np.float32), np.concatenate([s, -s]).astype(np.float32)


def _stack(rows, at_row):
    st = np.zeros((STK, rows.shape[1]), rows.dtype)
    for g in range(3):
        st[32 * g + at_row:32 * g + at_row + RANK] = rows
    return st


def kernel(x, ctx_4096, mask_BxSxS2_ff0, L0_attn_w1, L0_attn_w2, L0_attn_b2, L0_attn_sparse_mask,
           L0_xattn_wq, L0_xattn_wk, L0_xattn_wv, L0_xattn_wo, L0_ffn_w1q, L0_ffn_a1, L0_ffn_b1,
           L0_ffn_w3q, L0_ffn_a3, L0_ffn_b3, L0_ffn_w2q, L0_ffn_a2, L0_ffn_b2):
    import concourse.bacc as _bacc
    from concourse.bass_utils import run_bass_kernel_spmd as _run

    a = np.asarray
    f32 = a(x).dtype
    stream = np.empty((NCH, P, 512), f32)
    w1, w2t = a(L0_attn_w1), a(L0_attn_w2).T
    ctxT = a(ctx_4096).reshape(TOK, D).T
    for k in range(KC):
        stream[2 * k] = w1[k * P:(k + 1) * P]
        stream[2 * k + 1] = w2t[k * P:(k + 1) * P]
        for hf in range(2):
            stream[CH_A + 2 * k + hf] = ctxT[k * P:(k + 1) * P, hf * HALF:(hf + 1) * HALF]

    def heads(w):
        w = a(w)
        return w.reshape(KC, P, -1, P).transpose(2, 1, 0, 3).reshape(-1, P, KC * P)
    weights = {"k": heads(L0_xattn_wk), "q": heads(L0_xattn_wq), "v": heads(L0_xattn_wv),
               "o": a(L0_xattn_wo).reshape(QH, P, D)}
    for c in range(CH0, NCH):
        g, (kind, i) = place_of(c)
        stream[c] = weights[kind][{"k": g, "v": g + i}.get(kind, HG * g + i)]

    cosT, sinT = _rope_tables()
    sel = np.zeros((P, RANK, STK), np.float32)
    for r in range(RANK):
        sel[:, r, r::32] = 1.0
    ones = np.zeros((P, P), np.float32)
    ones[0:64:32] = 1.0
    consts = np.concatenate([np.eye(P, dtype=np.float32), cosT, sinT, ones, sel.reshape(P, -1),
                             np.full((P, B), -0.5, np.float32)], axis=1)
    b2 = np.zeros((64, D), f32)
    b2[0::32] = a(L0_attn_b2)
    a_cols = np.ascontiguousarray((_stack(a(L0_ffn_a1), 0)[:, :]).T)
    a3 = _stack(a(L0_ffn_a3), RANK).T
    for g in range(3):
        a_cols[:, 32 * g + RANK:32 * g + 2 * RANK] = a3[:, 32 * g + RANK:32 * g + 2 * RANK]
    a2 = a(L0_ffn_a2).reshape(RANK, 4, FQ)
    a2_cols = np.zeros((P, FT, 4, RANK), f32)
    for t in range(FT):
        rows = min(P, FQ - t * P)
        a2_cols[:rows, t] = a2[:, :, t * P:t * P + rows].transpose(2, 1, 0)
    arrays = {
        "stream": stream, "x": a(x), "mask": a(mask_BxSxS2_ff0), "consts": consts,
        "spmask": a(L0_attn_sparse_mask), "b2": b2,
        "w1q": a(L0_ffn_w1q).T, "w3q": a(L0_ffn_w3q).T, "w2q": a(L0_ffn_w2q).T,
        "a_cols": a_cols, "bg_rows": _stack(a(L0_ffn_b1).T, 0), "bu_rows": _stack(a(L0_ffn_b3).T, RANK),
        "a2_cols": a2_cols.reshape(P, FT * 4, RANK), "b2_rows": _stack(a(L0_ffn_b2).T, 0),
    }
    nc = _bacc.Bacc("TRN2", target_bir_lowering=False, num_devices=1)
    given, args = {}, []
    for name, v in arrays.items():
        v = np.ascontiguousarray(v)
        given[f"in_{name}"] = v
        args.append(nc.dram_tensor(f"in_{name}", v.shape, mybir.dt.from_np(v.dtype), kind="ExternalInput").ap())
    args.append(nc.dram_tensor("out", (B, S, D), F32, kind="ExternalOutput").ap())
    decoder_block(nc, *args)
    r = _run(nc, [given], core_ids=[0])
    return r.results[0]["out"]
```

```python
from contextlib import ExitStack

import numpy as np

import concourse.bass as bass
from concourse import mybir

F32 = mybir.dt.float32
F32R = mybir.dt.float32r
ALU = mybir.AluOpType
ACT = mybir.ActivationFunctionType
AX = mybir.AxisListType

P = 128
B, S, D = 8, 128, 512
KC = D // P
TOK = B * S
HALF = TOK // 2
QH, KV, DK = 32, 8, 128
HG = QH // KV
FF = 1376
FQ = FF // 4
FT = (FQ + P - 1) // P
EPS = 1e-5
RANK = 2
LORA_SCALE = 0.5
STK = 96
LOWEST = -3.4e38

SLOTS = KV * B
TE = HG + 1
CH_A, CH_CTX = 8, 8
CH0 = CH_A + CH_CTX
CH_PAIR, CH_EVEN = 20, 11
NCH = CH0 + KV // 2 * CH_PAIR
WK, WQ = 0, 1
WV = WQ + HG
RING = 4
LAG = 3
FIRST, BODY = 2, 16
TURNS = 3
SPLIT_AT = [[[0], [1], [2], [3], [4, 5], [6, 7], [8], [9, 10]],
            [[0], [1], [2], [3], [4], [5], [6], [7, 8]]]


def first_chunk(g):
    return CH0 + CH_PAIR * (g // 2) + CH_EVEN * (g % 2)


def place_of(c):
    p, i = (c - CH0) // CH_PAIR, (c - CH0) % CH_PAIR
    g, i = (2 * p, i) if i < CH_EVEN else (2 * p + 1, i - CH_EVEN)
    if i < WV:
        return g, ("k", 0) if i == WK else ("q", i - WQ)
    if g % 2 == 0 and i < WV + 2:
        return g, ("v", i - WV)
    return g, ("o", i - WV - 2 * (g % 2 == 0))


def tiles_of(n):
    if n == -1:
        return list(range(TE)) + [TE, TE + 1]
    half = {3: (n + 5) // 4, 0: (n + 4) // 4, 1: (n + 3) // 4, 2: (n + 2) // 4}[n % 4]
    if half >= 2 * KV:
        return []
    return [TE * half + e for e in {3: [0, 1], 0: [2], 1: [3], 2: [4]}[n % 4]]


def chunks_of(n):
    if n >= SLOTS - B:
        return []
    g = n // B + 1
    return [first_chunk(g) + i for i in SPLIT_AT[g % 2][n % B]]


def decoder_block(nc, stream, x, mask, consts, spmask, b2, w1q, w3q, w2q, a_cols, bg_rows, bu_rows,
                  a2_cols, b2_rows, out):
    with ExitStack() as ctx:
        def sem(name):
            return ctx.enter_context(nc.semaphore(name))

        def sb(scope, name, shape, dt=F32):
            return scope.enter_context(nc.sbuf_tensor(name, shape, dt))

        ps = ctx.enter_context(nc.psum_tensor("ps", [P, 8, 512], F32))
        xres = sb(ctx, "xres", [P, B, D])
        maskq = sb(ctx, "maskq", [P, B, S])
        cst = sb(ctx, "cst", [P, 4 * P + 2 * STK + B])
        stats = sb(ctx, "stats", [P, 2, 6])
        mv = sb(ctx, "mv", [P, 3, B, 2])
        vep = sb(ctx, "vep", [P, 3, B])
        rstd = sb(ctx, "rstd", [P, 3, B])
        mx = sb(ctx, "mx", [P, 2, HG])
        nmx = sb(ctx, "nmx", [P, 2, HG])
        rs = sb(ctx, "rs", [P, 2, HG])
        rc = sb(ctx, "rc", [P, 2, HG])
        table_out = sb(ctx, "table_out", [P, 3])
        scores = ps[:, 0:2, :].rearrange("p a (h i k) -> p (a h) i k", h=2, i=2)
        ident = cst[:, 0:P]
        cosT, sinT = cst[:, P:2 * P], cst[:, 2 * P:3 * P]
        ones_raw = cst[0:2 * 32, 3 * P:4 * P]
        sel_raw = cst[:, 4 * P:4 * P + 2 * STK]
        minus_half = cst[:, 4 * P + 2 * STK:4 * P + 2 * STK + B]

        r1 = ExitStack()
        xT_h = sb(r1, "xT_h", [P, KC, TOK], F32R)
        xT_l = sb(r1, "xT_l", [P, KC, TOK], F32R)
        wq_h = sb(r1, "wq_h", [P, HG, KC, P], F32R)
        wq_l = sb(r1, "wq_l", [P, HG, KC, P], F32R)
        wk_h = sb(r1, "wk_h", [P, KC, P], F32R)
        wk_l = sb(r1, "wk_l", [P, KC, P], F32R)
        r2 = ExitStack()
        stg = sb(r2, "stg", [P, RING, 512])
        cT_h = sb(r2, "cT_h", [P, KC, TOK], F32R)
        cT_l = sb(r2, "cT_l", [P, KC, TOK], F32R)
        wv_h = sb(r2, "wv_h", [P, KC, 2, P], F32R)
        wv_l = sb(r2, "wv_l", [P, KC, 2, P], F32R)
        r3 = ExitStack()
        w1_h = sb(r3, "w1_h", [P, KC, D], F32R)
        w1_l = sb(r3, "w1_l", [P, KC, D], F32R)
        w2_h = sb(r3, "w2_h", [P, KC, D], F32R)
        w2_l = sb(r3, "w2_l", [P, KC, D], F32R)
        spm = sb(r3, "spm", [P, KC, D])
        atf = sb(r3, "atf", [P, KC, D])
        b2_raw = sb(r3, "b2_raw", [64, D])
        gap_a = sb(r3, "gap_a", [P, 6 * 256])
        at_h = sb(r3, "at_h", [P, KC, D], F32R)
        at_l = sb(r3, "at_l", [P, KC, D], F32R)
        xn = sb(r3, "xn", [P, 2, D])
        yb = sb(r3, "yb", [P, 2, D])
        b2_s = sb(r3, "b2_s", [64, D], F32R)
        ones = sb(r3, "ones", [64, P], F32R)
        r3.close()
        r3 = ExitStack()
        wo_h = sb(r3, "wo_h", [P, 2, HG, 512], F32R)
        wo_l = sb(r3, "wo_l", [P, 2, HG, 512], F32R)
        qr = sb(r3, "qr", [P, 2, TE, HALF])
        rot = sb(r3, "rot", [P, 2, HALF])
        qs = sb(r3, "qs", [P, TE, 2, P], F32R)
        pr = sb(r3, "pr", [P, 2, HG, P])
        pT_h = sb(r3, "pT_h", [P, HG * P], F32R)
        pT_l = sb(r3, "pT_l", [P, HG * P], F32R)
        o_h = sb(r3, "o_h", [P, HG * P], F32R)
        o_l = sb(r3, "o_l", [P, HG * P], F32R)
        ve_h = sb(r3, "ve_h", [P, 2, P], F32R)
        ve_l = sb(r3, "ve_l", [P, 2, P], F32R)
        vo_h = sb(r3, "vo_h", [P, B, P], F32R)
        vo_l = sb(r3, "vo_l", [P, B, P], F32R)
        r3.close()
        r2.close()
        r1.close()
        r1 = ExitStack()
        g1_h = sb(r1, "g1_h", [P, FF], F32R)
        g1_l = sb(r1, "g1_l", [P, FF], F32R)
        g3_h = sb(r1, "g3_h", [P, FF], F32R)
        g3_l = sb(r1, "g3_l", [P, FF], F32R)
        g1_raw = sb(r1, "g1_raw", [P, FF])
        g3_raw = sb(r1, "g3_raw", [P, FF])
        a_raw = sb(r1, "a_raw", [P, KC, STK])
        a_h = sb(r1, "a_h", [P, KC, STK], F32R)
        a_l = sb(r1, "a_l", [P, KC, STK], F32R)
        bg_s = sb(r1, "bg_s", [STK, FF], F32R)
        u_s = sb(r1, "u_s", [STK, TOK], F32R)
        a2c = sb(r1, "a2c", [P, FT * 4, RANK])
        gap_1 = sb(r1, "gap_1", [P, 52 * 256 - 7 * FF - 3 * KC * STK - TOK - FT * 4 * RANK])
        r2 = ExitStack()
        bg_raw = sb(r2, "bg_raw", [STK, FF])
        bu_raw = sb(r2, "bu_raw", [STK, FF])
        bu_s = sb(r2, "bu_s", [STK, FF], F32R)
        xs_f = sb(r2, "xs_f", [P, HALF])
        xs_h = sb(r2, "xs_h", [P, TOK], F32R)
        xs_l = sb(r2, "xs_l", [P, TOK], F32R)
        xn3 = sb(r2, "xn3", [P, 2, D])
        xc_h = sb(r2, "xc_h", [P, KC, HALF], F32R)
        xc_l = sb(r2, "xc_l", [P, KC, HALF], F32R)
        gap_2 = sb(r2, "gap_2", [P, 48 * 256 - 3 * FF - HALF - 2 * TOK - 2 * D - 2 * KC * HALF])
        r3 = ExitStack()
        g2_raw = sb(r3, "g2_raw", [P, FT, D])
        bd_raw = sb(r3, "bd_raw", [STK, D])
        gs_h = sb(r3, "gs_h", [P, FT, HALF], F32R)
        v_s = sb(r3, "v_s", [STK, HALF], F32R)
        g2_h = sb(r3, "g2_h", [P, FT, D], F32R)
        bd_s = sb(r3, "bd_s", [STK, D], F32R)
        gs_l = sb(r3, "gs_l", [P, FT, HALF], F32R)
        sel = sb(r3, "sel", [P, RANK, STK], F32R)
        gap_3 = sb(r3, "gap_3", [P, 2 * 256 - RANK * STK])
        gsum = sb(r3, "gsum", [P, FT, HALF])
        lacc0 = sb(r3, "lacc0", [P, RANK + 1, HALF])
        sil = sb(r3, "sil", [P, 2, HALF])
        gate = sb(r3, "gate", [P, 2, HALF])
        prod = sb(r3, "prod", [P, HALF])
        g2_l = sb(r3, "g2_l", [P, FT, D], F32R)
        lo_h = sb(r3, "lo_h", [P, RANK, HALF], F32R)
        lo_l = sb(r3, "lo_l", [P, RANK, HALF], F32R)
        ost = sb(r3, "ost", [P, 4, D])
        lacc1 = sb(r3, "lacc1", [P, RANK + 1, HALF])
        lacc = [lacc0, lacc1]
        r3.close()
        r2.close()
        r1.close()
        del gap_a, gap_1, gap_2, gap_3

        in_cst, in_b2, in_spm, in_mask = sem("in_cst"), sem("in_b2"), sem("in_spm"), sem("in_mask")
        in_x = [sem(f"in_x{b}") for b in range(B)]
        in_stg = [sem(f"in_stg{r}") for r in range(RING)]
        chunk_hi, chunk_lo, wlo = sem("chunk_hi"), sem("chunk_lo"), sem("wlo")
        agg, vepd, powd, xnd = sem("agg"), sem("vepd"), sem("powd"), sem("xnd")
        bns = sem("bns")
        wprod, attd, at_hid, at_lod = sem("wprod"), sem("attd"), sem("at_hid"), sem("at_lod")
        tr, tr_hi, tr_lo = sem("tr"), sem("tr_hi"), sem("tr_lo")
        ymm, gel, x1d, ones_d, b2_hi, b2_lo = (sem("ymm"), sem("gel"), sem("x1d"), sem("ones_d"),
                                               sem("b2_hi"), sem("b2_lo"))
        tile_mm, rope_mul, rope_add = sem("tile_mm"), sem("rope_mul"), sem("rope_add")
        q_hi, q_lo = sem("q_hi"), sem("q_lo")
        mask_added = sem("mask_added")
        scored, masked, maxed, expd, recd, normd = (sem("scored"), sem("masked"), sem("maxed"),
                                                    sem("expd"), sem("recd"), sem("normd"))
        pT, pT_hid, pT_lod = sem("pT"), sem("pT_hid"), sem("pT_lod")
        vmm, v_hid, v_lod = sem("vmm"), sem("v_hid"), sem("v_lod")
        pv, o_hid, o_lod = sem("pv"), sem("o_hid"), sem("o_lod")
        womm, accd = sem("womm"), sem("accd")
        in_ff = [sem(f"in_ff{i}") for i in range(4)]
        a_hi, a_lo, g_hi, g_lo = sem("a_hi"), sem("a_lo"), sem("g_hi"), sem("g_lo")
        bs_hi, bg_lod, bu_lod = sem("bs_hi"), sem("bg_lod"), sem("bu_lod")
        g2_hi, g2_lo = sem("g2_hi"), sem("g2_lo")
        bd_hi, bd_lo, seld = sem("bd_hi"), sem("bd_lo"), sem("seld")
        t3, t3_hi, t3_lo, xsum = sem("t3"), sem("t3_hi"), sem("t3_lo"), sem("xsum")
        xs_hid, xs_lod = sem("xs_hid"), sem("xs_lod")
        umm, u_hid, u_lod = sem("umm"), sem("u_hid"), sem("u_lod")
        gu, sild, gated, gsd, gs_hid, gs_lod = (sem("gu"), sem("sild"), sem("gated"), sem("gsd"),
                                                sem("gs_hid"), sem("gs_lod"))
        l_dve, prodd, l_pool, l_sum = sem("l_dve"), sem("prodd"), sem("l_pool"), sem("l_sum")
        l_hid, l_lod, vm, v3_hi, v3_lo = (sem("l_hid"), sem("l_lod"), sem("vm"), sem("v3_hi"),
                                          sem("v3_lo"))
        down, outd, stored = sem("down"), sem("outd"), [sem(f"stored{i}") for i in range(4)]

        def three(pe, dst, a_hi, a_lo, b_hi, b_lo, first, last):
            pe.matmul(dst, a_hi, b_hi, start=first, stop=False)
            pe.matmul(dst, a_hi, b_lo, start=False, stop=False)
            return pe.matmul(dst, a_lo, b_hi, start=False, stop=last)

        def f(ap):
            return ap.bitcast(F32)

        def at(value, per_turn, turn):
            return value if turn is None else turn * per_turn + value

        def chunk_dst(c):
            if c < CH_A:
                hi, lo = (w2_h, w2_l) if c % 2 else (w1_h, w1_l)
                return hi[:, c // 2], lo[:, c // 2]
            if c < CH0:
                k, hf = (c - CH_A) // 2, (c - CH_A) % 2
                cols = slice(hf * HALF, (hf + 1) * HALF)
                return cT_h[:, k, cols], cT_l[:, k, cols]
            g, (kind, i) = place_of(c)
            if kind == "v":
                return wv_h[:, :, i, :], wv_l[:, :, i, :]
            if kind == "o":
                return wo_h[:, g % 2, i, :], wo_l[:, g % 2, i, :]
            pair = (wk_h[:], wk_l[:]) if kind == "k" else (wq_h[:, i], wq_l[:, i])
            return tuple(p.rearrange("p k c -> p (k c)") for p in pair)

        def chunk_src(c):
            src = stg[:, c % RING, :]
            if c >= CH0 and place_of(c)[1][0] == "v":
                return src.rearrange("p (k c) -> p k c", k=KC)
            return src

        def values_of(n):
            b = n % B
            return (vo_h[:, b, :], vo_l[:, b, :]) if n // B % 2 else (ve_h[:, b % 2, :], ve_l[:, b % 2, :])

        def makes_values(n):
            return n < SLOTS and n // B % 2 == 0

        def value_count(n):
            return B * (n // (2 * B)) + (n % B + 1 if n // B % 2 == 0 else B)

        turns_a = [(1, 0), (1, 1)]
        for b in range(B + LAG):
            turns_a += [(1, b + 2)] * (b + 2 < B) + [(2, b - LAG)] * (b >= LAG)
        place_a = {t: i for i, t in enumerate(turns_a)}

        early_tiles = {B - 1: [0], B: [1, 2], B + 1: [3, 4], B + 2: [5, 6]}
        PRE = 4

        def early_chunks(b):
            rest, steps = CH0 + CH_EVEN - CH_A - PRE, B + LAG - 1
            return range(CH_A + PRE + rest * min(b, steps) // steps,
                         CH_A + PRE + rest * min(b + 1, steps) // steps)

        UPS = FT * 4
        TAIL = SLOTS - B + 2

        table_col = {ACT.Gelu: 0, ACT.Exp: 1, ACT.Silu: 2}
        t3_bank = [7, 2, 7, 2, 7, 7, 7, 7]
        down_bank = [4, 5, 7, 4, 5, 7, 4, 0]

        def up_of(i):
            t = i % UPS // 4
            return i // UPS, t, i % 4, min(P, FQ - t * P)

        def weighed(i):
            return 3 * (i // 2) + 2 + i % 2

        loop_slots = range(FIRST, FIRST + BODY)
        tail_slots = range(FIRST + BODY * TURNS, SLOTS + 2)
        TPT, CPT, VPT = TE * BODY // 4, CH_PAIR, B

        block = ctx.enter_context(nc.Block())

        @block.sync
        def _(sp):
            def load_chunk(c, turn=None, src=None):
                if c >= RING:
                    if c - RING < CH_A:
                        sp.wait_ge(wlo, c - RING + 1)
                    else:
                        sp.wait_ge(chunk_lo, at(c - RING - CH_A + 1, RING, turn))
                sp.dma_start(stg[:, c % RING, :], stream[c] if src is None else src)\
                  .then_inc(in_stg[c % RING], 16)

            for c in range(RING):
                load_chunk(c)
            sp.dma_start(cst[:], consts).then_inc(in_cst, 16)
            for b in range(2):
                sp.dma_start(xres[:, b, :], x[b]).then_inc(in_x[b], 16)
            for c in range(RING, CH_A):
                load_chunk(c)
            sp.dma_start(b2_raw[:], b2).then_inc(in_b2, 16)
            for b in range(2, 4):
                sp.dma_start(xres[:, b, :], x[b]).then_inc(in_x[b], 16)
            sp.dma_start(spm[:], spmask.rearrange("(m p) t -> p m t", p=P)).then_inc(in_spm, 16)
            for b in range(4, B):
                sp.dma_start(xres[:, b, :], x[b]).then_inc(in_x[b], 16)
            sp.dma_start(maskq[:], mask.rearrange("b q k -> q b k")).then_inc(in_mask, 16)
            for c in range(CH_A, 4 * RING):
                load_chunk(c)
            with sp.Fori(0, (NCH - 4 * RING) // RING) as turn:
                for r in range(RING):
                    place = sp.snap(turn * RING + (4 * RING + r))
                    load_chunk(4 * RING + r, turn, stream[bass.ds(place, 1)].rearrange("a p n -> (a p) n"))
            sp.wait_ge(tile_mm, TE * 2 * KV)
            sp.wait_ge(vmm, SLOTS // 2)
            sp.wait_ge(chunk_lo, NCH - CH_A)
            sp.dma_start(a_raw[:], a_cols.rearrange("(k p) c -> p k c", p=P)).then_inc(in_ff[0], 16)
            sp.dma_start(g1_raw[:], w1q).then_inc(in_ff[0], 16)
            sp.dma_start(g3_raw[:], w3q).then_inc(in_ff[0], 16)
            sp.dma_start(bg_raw[:], bg_rows).then_inc(in_ff[1], 16)
            sp.dma_start(bu_raw[:], bu_rows).then_inc(in_ff[1], 16)
            sp.dma_start(a2c[:], a2_cols).then_inc(in_ff[3], 16)
            sp.wait_ge(womm, SLOTS - B)
            sp.dma_start(g2_raw[:, 0:FT - 1, :], w2q[0:(FT - 1) * P].rearrange("(t p) n -> p t n", p=P))\
              .then_inc(in_ff[2], 16)
            sp.dma_start(g2_raw[0:FQ - (FT - 1) * P, FT - 1, :], w2q[(FT - 1) * P:FQ]).then_inc(in_ff[2], 16)
            sp.dma_start(bd_raw[:], b2_rows).then_inc(in_ff[2], 16)
            for b in range(B):
                sp.wait_ge(outd, b + 1)
                sp.dma_start(out[b], ost[:, b % 4, :]).then_inc(stored[b % 4], 16)
            for r in range(4):
                sp.wait_ge(stored[r], 16 * B // 4)

        @block.tensor
        def _(pe):
            for k in range(KC):
                pe.wait_ge(chunk_hi, 2 * k + 2)
                pe.wait_ge(wlo, 2 * k + 2)
                for m in range(KC):
                    cols = slice(m * P, (m + 1) * P)
                    mm = three(pe, ps[:, m, :], w1_h[:, k, cols], w1_l[:, k, cols],
                               w2_h[:, k, :], w2_l[:, k, :], k == 0, k == KC - 1)
                    if k == KC - 1:
                        mm.then_inc(wprod, 1)

            def transpose_a(norm, b):
                i = place_a[norm, b]
                pe.wait_ge(xnd, i + 1)
                if i >= 2:
                    pe.wait_ge(tr_lo, i - 1)
                for k in range(KC):
                    mm = pe.transpose(ps[:, 4 + i % 2, k * P:(k + 1) * P],
                                      xn[:, i % 2, k * P:(k + 1) * P], ident)
                mm.then_inc(tr, 1)

            def project(t, turn):
                half, e = t // TE, t % TE
                g = half // 2
                pe.wait_ge(chunk_lo, at(first_chunk(g) + e - CH_A + 1, CPT, turn))
                if t < 2 * TE and e:
                    pe.wait_ge(tr_lo, place_a[2, 4 * half + 3] + 1)
                if t >= 2:
                    pe.wait_ge(rope_mul, at(t - 1, TPT, turn))
                cols = slice((half % 2) * HALF, (half % 2 + 1) * HALF)
                for k in range(KC):
                    if e == 0:
                        mm = three(pe, ps[:, 2 + t % 2, :], wk_h[:, k, :], wk_l[:, k, :],
                                   cT_h[:, k, cols], cT_l[:, k, cols], k == 0, k == KC - 1)
                    else:
                        mm = three(pe, ps[:, 2 + t % 2, :], wq_h[:, e - 1, k, :], wq_l[:, e - 1, k, :],
                                   xT_h[:, k, cols], xT_l[:, k, cols], k == 0, k == KC - 1)
                mm.then_inc(tile_mm, 1)

            pe.wait_ge(in_cst, 16)
            transpose_a(1, 0)
            transpose_a(1, 1)
            for b in range(B + LAG):
                if 0 < b and b + 2 < B:
                    transpose_a(1, b + 2)
                if b >= LAG:
                    transpose_a(2, b - LAG)
                if b < B:
                    pe.wait_ge(tr_lo, place_a[1, b] + 1)
                    if b >= 2:
                        pe.wait_ge(gel, b - 1)
                    cols = slice(b * S, (b + 1) * S)
                    for k in range(KC):
                        if b == 0:
                            pe.wait_ge(at_lod, k + 1)
                        three(pe, ps[:, 6 + b % 2, :], xT_h[:, k, cols], xT_l[:, k, cols],
                              at_h[:, k, :], at_l[:, k, :], k == 0, False)
                    if b == 0:
                        pe.wait_ge(b2_lo, 1)
                    pe.matmul(ps[:, 6 + b % 2, :], ones[:], b2_s[:], start=False, stop=True)\
                      .then_inc(ymm, 1)
                if b == 0:
                    transpose_a(1, 2)
                for t in early_tiles.get(b, []):
                    project(t, None)

            def transpose_c(b):
                pe.wait_ge(xnd, len(turns_a) + b + 1)
                last = b if b > 4 else b - 1
                if last > 0:
                    pe.wait_ge(xsum, last)
                for k in range(KC):
                    mm = pe.transpose(ps[:, t3_bank[b], k * P:(k + 1) * P],
                                      xn3[:, b % 2, k * P:(k + 1) * P], ident)
                mm.then_inc(t3, 1)

            def slot(n, turn=None):
                b, g = n % B, n // B
                if n < SLOTS:
                    pe.wait_ge(q_lo, at(n + 1, BODY, turn))
                    if n >= 1:
                        pe.wait_ge(masked, at(n, BODY, turn))
                    for h in range(HG):
                        dst = ps[:, h // 2, h % 2 * 2 * P:(h % 2 + 1) * 2 * P]
                        pe.matmul(dst, qs[:, 1 + h, 0, :], qs[:, 0].rearrange("p a c -> p (a c)"),
                                  start=True, stop=False)
                        mm = pe.matmul(dst[:, 0:P], qs[:, 1 + h, 1, :], qs[:, 0, 0, :],
                                       start=False, stop=True)
                    mm.then_inc(scored, 1)
                for t in tiles_of(n):
                    project(t, turn)
                if 1 <= n <= SLOTS:
                    pe.wait_ge(normd, at(n, BODY, turn))
                    if n >= 2:
                        pe.wait_ge(pT_lod, at(n - 1, BODY, turn))
                    for h in range(HG):
                        mm = pe.transpose(ps[:, 4, h * P:(h + 1) * P], pr[:, (n - 1) % 2, h, :], ident)
                    mm.then_inc(pT, 1)
                if n >= 2:
                    m = n - 2
                    pe.wait_ge(o_lod, at(m + 1, BODY, turn))
                    pe.wait_ge(chunk_lo, at(first_chunk(m // B + 1) - CH_A, CPT, turn))
                    if m >= 1:
                        pe.wait_ge(accd, at(m, BODY, turn))
                    for h in range(HG):
                        cols = slice(h * P, (h + 1) * P)
                        mm = three(pe, ps[:, 6, :], o_h[:, cols], o_l[:, cols],
                                   wo_h[:, (m // B) % 2, h, :], wo_l[:, (m // B) % 2, h, :],
                                   h == 0, h == HG - 1)
                    mm.then_inc(womm, 1)
                if TAIL + 2 <= n <= SLOTS:
                    transpose_c(n - TAIL - 2)
                if makes_values(n):
                    pe.wait_ge(chunk_lo, at(first_chunk(g) + WV + 2 - CH_A, CPT, turn))
                    if n >= 1:
                        pe.wait_ge(v_lod, at(value_count(n) - 1, VPT, turn))
                    cols = slice(b * S, (b + 1) * S)
                    for k in range(KC):
                        mm = three(pe, ps[:, 7, 0:2 * P], cT_h[:, k, cols], cT_l[:, k, cols],
                                   wv_h[:, k].rearrange("p g c -> p (g c)"),
                                   wv_l[:, k].rearrange("p g c -> p (g c)"), k == 0, k == KC - 1)
                    mm.then_inc(vmm, 1)
                if 1 <= n <= SLOTS:
                    m = n - 1
                    pe.wait_ge(pT_lod, at(m + 1, BODY, turn))
                    pe.wait_ge(v_lod, at(value_count(m), VPT, turn))
                    if m >= 1:
                        pe.wait_ge(o_lod, at(m, BODY, turn))
                    three(pe, ps[:, 5, :], *values_of(m), pT_h[:], pT_l[:], True, True).then_inc(pv, 1)

            def lora_in(hf):
                pe.wait_ge(a_lo, 1)
                pe.wait_ge(t3_lo, 4 * hf + 4)
                for k in range(KC):
                    mm = three(pe, ps[0:STK, 3 + hf, :], a_h[:, k, :], a_l[:, k, :],
                               xc_h[:, k, :], xc_l[:, k, :], k == 0, k == KC - 1)
                mm.then_inc(umm, 1)

            def up(i):
                hf, t, j, rows = up_of(i)
                cols = slice(j * FQ + t * P, j * FQ + t * P + rows)
                toks = slice(hf * HALF, (hf + 1) * HALF)
                if i == 0:
                    pe.wait_ge(g_lo, 4)
                if i % UPS == 0:
                    pe.wait_ge(xs_lod, hf + 1)
                if i >= 2:
                    pe.wait_ge(gated, i - 1)
                halves = ((0, g1_h, g1_l, bg_s, bg_lod), (1, g3_h, g3_l, bu_s, bu_lod))
                for s, w_h, w_l, _, _ in halves:
                    three(pe, ps[0:rows, 2 * s + i % 2, :], w_h[:, cols], w_l[:, cols], xs_h[:, toks],
                          xs_l[:, toks], True, False)
                if i % UPS == 0:
                    pe.wait_ge(u_lod, hf + 1)
                for s, _, _, rows_s, parts in halves:
                    if i == 0:
                        pe.wait_ge(parts, 1)
                    mm = pe.matmul(ps[0:rows, 2 * s + i % 2, :], rows_s[:, cols], u_s[:, toks],
                                   start=False, stop=True)
                mm.then_inc(gu, 1)

            def lora_out(hf):
                pe.wait_ge(seld, 1)
                pe.wait_ge(l_lod, hf + 1)
                if hf == 1:
                    pe.wait_ge(v3_lo, 1)
                for r in range(RANK):
                    pe.matmul(ps[0:STK, 6, :], sel[:, r, :], lo_h[:, r, :], start=(r == 0), stop=False)
                    mm = pe.matmul(ps[0:STK, 6, :], sel[:, r, :], lo_l[:, r, :], start=False,
                                   stop=(r == RANK - 1))
                mm.then_inc(vm, 1)

            def down_rows(b, t):
                if t == 0:
                    if b == 0:
                        pe.wait_ge(g2_lo, 1)
                    if 3 <= b < B - 1:
                        pe.wait_ge(outd, b - 2)
                    if b == B - 1:
                        pe.wait_ge(gated, 2 * UPS - 1)
                pe.wait_ge(gs_lod, FT * (b // 4) + t + 1)
                rows = min(P, FQ - t * P)
                cols = slice((b % 4) * S, (b % 4 + 1) * S)
                three(pe, ps[:, down_bank[b], :], gs_h[0:rows, t, cols], gs_l[0:rows, t, cols],
                      g2_h[0:rows, t, :], g2_l[0:rows, t, :], t == 0, False)

            def down_lora(b):
                pe.wait_ge(bd_lo, 1)
                pe.wait_ge(v3_lo, b // 4 + 1)
                cols = slice((b % 4) * S, (b % 4 + 1) * S)
                pe.matmul(ps[:, down_bank[b], :], v_s[:, cols], bd_s[:], start=False, stop=True)\
                  .then_inc(down, 1)

            for n in range(FIRST):
                slot(n)
            with pe.Fori(0, TURNS) as turn:
                for n in loop_slots:
                    slot(n, turn)
            for n in tail_slots:
                slot(n)
                if n == SLOTS:
                    lora_in(0)
            up(0)
            up(1)
            transpose_c(B - 3)
            for i in range(2, UPS):
                up(i)
                if i == 3:
                    transpose_c(B - 2)
                if i == 5:
                    transpose_c(B - 1)
                if i == 7:
                    lora_in(1)
            for i in range(UPS, 2 * UPS):
                up(i)
                if i == UPS + 4:
                    lora_out(0)
                if i == UPS + 5:
                    for b in range(4):
                        for t in range(FT):
                            down_rows(b, t)
                        down_lora(b)
            for t in range(FT):
                for b in range(4, B):
                    down_rows(b, t)
                    if t == FT - 1 and b == 5:
                        lora_out(1)
            for b in range(4, B):
                down_lora(b)

        @block.scalar
        def _(act):
            def chunk(c, turn=None):
                act.wait_ge(in_stg[c % RING], at(16 * (c // RING + 1), 16 * CPT // RING, turn))
                if c >= CH0:
                    g, (kind, i) = place_of(c)
                    if kind in "kq" and g >= 1:
                        e = 0 if kind == "k" else 1 + i
                        act.wait_ge(tile_mm, at(TE * (2 * g - 1) + e + 1, TPT, turn))
                    elif kind == "v" and g >= 2:
                        act.wait_ge(vmm, at(B * (g // 2), VPT, turn))
                    elif kind == "o" and g >= 2:
                        act.wait_ge(womm, at(B * (g - 1), BODY, turn))
                    elif kind == "o":
                        act.wait_ge(wprod, KC)
                act.copy(chunk_dst(c)[0], chunk_src(c)).then_inc(chunk_hi, 1)

            def load_table(function):
                act.activation(table_out[:, table_col[function]:table_col[function] + 1], minus_half[:, 0:1],
                               function)

            for c in range(CH_A):
                chunk(c)
            act.wait_ge(in_cst, 16)
            act.copy(ones[:], ones_raw).then_inc(ones_d, 1)
            load_table(ACT.Gelu)
            act.wait_ge(in_b2, 16)
            act.wait_ge(ones_d, 1)
            act.copy(b2_s[:], b2_raw[:]).then_inc(b2_hi, 1)
            for m in range(KC):
                act.wait_ge(attd, m + 1)
                act.copy(at_h[:, m, :], atf[:, m, :]).then_inc(at_hid, 1)

            def split_a(norm, b):
                i = place_a[norm, b]
                act.wait_ge(tr, i + 1)
                act.copy(xT_h[:, :, b * S:(b + 1) * S],
                         ps[:, 4 + i % 2, :].rearrange("p (k t) -> p k t", k=KC)).then_inc(tr_hi, 1)

            split_a(1, 0)
            split_a(1, 1)
            for c in range(CH_A, CH_A + PRE):
                chunk(c)
            for b in range(B + LAG):
                if b + 2 < B:
                    split_a(1, b + 2)
                if b >= LAG:
                    split_a(2, b - LAG)
                for c in early_chunks(b):
                    chunk(c)
                if b < B:
                    act.wait_ge(ymm, b + 1)
                    if b >= 2:
                        act.wait_ge(x1d, b - 1)
                    act.activation(yb[:, b % 2, :], ps[:, 6 + b % 2, :], ACT.Gelu).then_inc(gel, 1)

            def split_q(n, turn):
                act.wait_ge(rope_add, at(TE * (n // 4) + TE, TPT, turn))
                if n >= 1:
                    act.wait_ge(scored, at(n, BODY, turn))
                act.copy(qs[:, :, 0, :], qr[:, (n // 4) % 2, :, (n % 4) * P:(n % 4 + 1) * P]).then_inc(q_hi, 1)

            def split_c(b):
                act.wait_ge(t3, b + 1)
                if b >= 4:
                    act.wait_ge(umm, 1)
                act.copy(xc_h[:, :, (b % 4) * S:(b % 4 + 1) * S],
                         ps[:, t3_bank[b], :].rearrange("p (k t) -> p k t", k=KC)).then_inc(t3_hi, 1)

            def split_p(m, turn):
                act.wait_ge(pT, at(m + 1, BODY, turn))
                if m >= 1:
                    act.wait_ge(pv, at(m, BODY, turn))
                act.copy(pT_h[:], ps[:, 4, :]).then_inc(pT_hid, 1)

            def weights_hi(n):
                if n == TAIL + 2:
                    act.wait_ge(in_ff[0], 3 * 16)
                    act.copy(a_h[:], a_raw[:]).then_inc(a_hi, 1)
                    act.copy(g1_h[:], g1_raw[:]).then_inc(g_hi, 1)
                if n == TAIL + 3:
                    act.copy(g3_h[:], g3_raw[:]).then_inc(g_hi, 1)
                if n == TAIL + 4:
                    act.wait_ge(in_ff[1], 2 * 16)
                    act.copy(bg_s[:], bg_raw[:]).then_inc(bs_hi, 1)
                if n == SLOTS:
                    act.copy(bu_s[:], bu_raw[:]).then_inc(bs_hi, 1)
                    act.wait_ge(womm, SLOTS - B)
                    act.wait_ge(in_ff[2], 3 * 16)
                    act.copy(bd_s[:], bd_raw[:]).then_inc(bd_hi, 1)
                    act.copy(g2_h[:, 0:FT - 1, :], g2_raw[:, 0:FT - 1, :])
                    act.copy(g2_h[0:FQ - (FT - 1) * P, FT - 1, :], g2_raw[0:FQ - (FT - 1) * P, FT - 1, :])\
                       .then_inc(g2_hi, 1)

            def slot(n, turn=None):
                if n >= 2:
                    m = n - 2
                    act.wait_ge(pv, at(m + 1, BODY, turn))
                    if m >= 1:
                        act.wait_ge(womm, at(m, BODY, turn))
                    act.copy(o_h[:], ps[:, 5, :]).then_inc(o_hid, 1)
                if TAIL + 3 <= n <= SLOTS:
                    split_c(n - TAIL - 3)
                if n + 1 < SLOTS:
                    split_q(n + 1, turn)
                if 1 <= n <= SLOTS:
                    split_p(n - 1, turn)
                if n >= TAIL + 3:
                    weights_hi(n)
                if n < SLOTS:
                    act.wait_ge(maxed, at(n + 1, BODY, turn))
                    for h in range(HG):
                        last = act.activation(pr[:, n % 2, h, :], pr[:, n % 2, h, :], ACT.Exp,
                                              bias=nmx[:, n % 2, h:h + 1], scale=1.0,
                                              accum_out=rs[:, n % 2, h:h + 1])
                    last.then_inc(expd, 1)
                if n == TAIL + 2:
                    weights_hi(n)
                for c in chunks_of(n):
                    chunk(c, turn)
                if makes_values(n):
                    act.wait_ge(vmm, at(value_count(n), VPT, turn))
                    if n >= 2:
                        act.wait_ge(pv, at(n - 1, BODY, turn))
                    act.copy(values_of(n)[0], ps[:, 7, 0:P])
                    act.copy(values_of(n + B)[0], ps[:, 7, P:2 * P]).then_inc(v_hid, 1)

            def split_sum(hf):
                cols = slice(hf * HALF, (hf + 1) * HALF)
                act.wait_ge(xsum, 4 * hf + 4)
                act.copy(xs_h[:, cols], xs_f[:]).then_inc(xs_hid, 1)
                act.wait_ge(umm, hf + 1)
                act.mul(u_s[:, cols], ps[0:STK, 3 + hf, :], LORA_SCALE).then_inc(u_hid, 1)

            def silu(i):
                hf, t, j, rows = up_of(i)
                act.wait_ge(gu, i + 1)
                if i >= 2:
                    act.wait_ge(gated, i - 1)
                act.activation(sil[0:rows, i % 2, :], ps[0:rows, i % 2, :], ACT.Silu).then_inc(sild, 1)

            def weigh(i):
                hf, t, j, rows = up_of(i)
                act.wait_ge(gated, i + 1)
                if i % UPS == 1:
                    dst = lacc[hf][0:rows, RANK, :]
                else:
                    if i >= 5:
                        act.wait_ge(l_pool, i // 2 - 1 - hf)
                    dst = prod[0:rows, :]
                act.activation(dst, gate[0:rows, i % 2, :], ACT.Copy, scale=a2c[0:rows, t * 4 + j, 1:2])\
                   .then_inc(prodd, 1)

            def split_gs(hf, t):
                rows = min(P, FQ - t * P)
                act.wait_ge(gsd, (hf * FT + t + 1) * 3)
                if hf == 1:
                    act.wait_ge(down, 4)
                elif t == 0:
                    act.wait_ge(womm, SLOTS)
                act.copy(gs_h[0:rows, t, :], gsum[0:rows, t, :]).then_inc(gs_hid, 1)

            def split_lora(hf):
                act.wait_ge(l_sum, hf + 1)
                if hf == 1:
                    act.wait_ge(vm, 1)
                act.copy(lo_h[:], lacc[hf][:, 0:RANK, :]).then_inc(l_hid, 1)

            def split_v(hf):
                act.wait_ge(vm, hf + 1)
                if hf == 1:
                    act.wait_ge(down, 4)
                act.mul(v_s[:], ps[0:STK, 6, :], LORA_SCALE).then_inc(v3_hi, 1)

            load_table(ACT.Exp)
            split_q(0, None)
            for n in range(FIRST):
                slot(n)
            with act.Fori(0, TURNS) as turn:
                for n in loop_slots:
                    slot(n, turn)
            for n in tail_slots:
                slot(n)
            split_sum(0)
            split_c(4)
            load_table(ACT.Silu)
            act.wait_ge(in_ff[3], 16)
            for i in range(2 * UPS):
                silu(i)
                if i % 2 and i < 2 * UPS - 1:
                    weigh(i)
                if i == 1:
                    split_c(5)
                if i == 3:
                    split_c(6)
                if i == 5:
                    split_c(7)
                if i == 7:
                    split_sum(1)
                    act.copy(sel[:], sel_raw.rearrange("p (r c) -> p r c", r=RANK)).then_inc(seld, 1)
                if i == UPS + 2:
                    split_lora(0)
                if i == UPS + 4:
                    split_v(0)
                if i == UPS + 5:
                    split_gs(1, 0)
                elif i % 4 == 0 and i and i != UPS + 4:
                    split_gs((i // 4 - 1) // FT, (i // 4 - 1) % FT)
            split_gs(1, FT - 1)
            split_lora(1)
            split_v(1)

        @block.vector
        def _(dve):
            def norm_stats(norm, b):
                i = norm * B + b
                if i >= 2:
                    dve.wait_ge(agg, i - 1)
                dve.bn_stats(stats[:, i % 2, :], xres[:, b, :]).then_inc(bns, 1)
                dve.wait_ge(bns, i + 1)
                dve.bn_aggr(mv[:, norm, b, :], stats[:, i % 2, :]).then_inc(agg, 1)
                dve.wait_ge(agg, i + 1)
                dve.tensor_scalar(vep[:, norm, b:b + 1], mv[:, norm, b, 1:2], EPS, None, ALU.add)\
                   .then_inc(vepd, 1)

            def apply_norm(dst, norm, b):
                return dve.tensor_scalar(dst, xres[:, b, :], mv[:, norm, b, 0:1],
                                         rstd[:, norm, b:b + 1], ALU.subtract, ALU.mult)

            def norm_a(norm, b):
                i = place_a[norm, b]
                dve.wait_ge(powd, b // 2 + 1 if norm == 1 else B // 2 + b + 1)
                if i >= 2:
                    dve.wait_ge(tr, i - 1)
                apply_norm(xn[:, i % 2, :], norm - 1, b).then_inc(xnd, 1)

            def split_a(norm, b):
                i = place_a[norm, b]
                cols = slice(b * S, (b + 1) * S)
                dve.wait_ge(tr_hi, i + 1)
                dve.tensor_tensor(xT_l[:, :, cols], ps[:, 4 + i % 2, :].rearrange("p (k t) -> p k t", k=KC),
                                  f(xT_h[:, :, cols]), ALU.subtract).then_inc(tr_lo, 1)

            for c in range(CH_A):
                dve.wait_ge(chunk_hi, c + 1)
                hi, lo = chunk_dst(c)
                dve.tensor_tensor(lo, stg[:, c % RING, :], f(hi), ALU.subtract).then_inc(wlo, 1)
                if c in (3, 4):
                    dve.wait_ge(in_x[c - 3], 16)
                    norm_stats(0, c - 3)
            norm_a(1, 0)
            norm_a(1, 1)
            for b in range(2, 4):
                dve.wait_ge(in_x[b], 16)
                norm_stats(0, b)
            dve.wait_ge(b2_hi, 1)
            dve.tensor_tensor(b2_s[32:64, :], b2_raw[32:64, :], f(b2_s[32:64, :]), ALU.subtract)\
               .then_inc(b2_lo, 1)
            dve.wait_ge(in_spm, 16)
            for m in range(KC):
                dve.wait_ge(wprod, m + 1)
                dve.tensor_tensor(atf[:, m, :], ps[:, m, :], spm[:, m, :], ALU.mult).then_inc(attd, 1)
            for m in range(KC):
                dve.wait_ge(at_hid, m + 1)
                dve.tensor_tensor(at_l[:, m, :], atf[:, m, :], f(at_h[:, m, :]), ALU.subtract)\
                   .then_inc(at_lod, 1)
                if m == 1:
                    split_a(1, 0)
            norm_a(1, 2)
            split_a(1, 1)

            def rope(t, turn):
                half, e = t // TE, t % TE
                dve.wait_ge(tile_mm, at(t + 1, TPT, turn))
                if half >= 2:
                    dve.wait_ge(q_lo, at(4 * half - 4, BODY, turn))
                if t >= 2:
                    dve.wait_ge(rope_add, at(t - 1, TPT, turn))
                src = ps[:, 2 + t % 2, :].rearrange("p (b s) -> p b s", b=4)
                dst = rot[:, t % 2, :].rearrange("p (b s) -> p b s", b=4)
                h = DK // 2

                def table(lo, hi, tab):
                    return tab[lo:hi, :].rearrange("p (a s) -> p a s", a=1).to_broadcast([hi - lo, 4, S])
                dve.tensor_tensor(qr[:, half % 2, e, :].rearrange("p (b s) -> p b s", b=4), src,
                                  table(0, DK, cosT), ALU.mult)
                dve.tensor_tensor(dst[0:h], src[h:DK], table(h, DK, sinT), ALU.mult)
                dve.tensor_tensor(dst[h:DK], src[0:h], table(0, h, sinT), ALU.mult).then_inc(rope_mul, 1)

            for b in range(B + LAG):
                if b >= LAG:
                    norm_a(2, b - LAG)
                for t in early_tiles.get(b - 1, [])[:1]:
                    rope(t, None)
                if b == 0:
                    norm_a(1, 3)
                if b < 2:
                    for i in (4 + 2 * b, 5 + 2 * b):
                        dve.wait_ge(in_x[i], 16)
                        norm_stats(0, i)
                if b + 2 < B:
                    split_a(1, b + 2)
                if b >= LAG:
                    split_a(2, b - LAG)
                for t in early_tiles.get(b - 1, [])[1:]:
                    rope(t, None)
                if 1 <= b and b + 3 < B:
                    norm_a(1, b + 3)
                if 1 <= b <= B:
                    dve.wait_ge(x1d, b)
                    norm_stats(1, b - 1)
            for t in early_tiles[B + LAG - 1]:
                rope(t, None)

            def stack_lo(stk, raw, src, count, done):
                dve.wait_ge(src, count)
                dve.tensor_tensor(stk[64:STK, :], raw[64:STK, :], f(stk[64:STK, :]), ALU.subtract)\
                   .then_inc(done, 1)

            def split_sum(hf):
                cols = slice(hf * HALF, (hf + 1) * HALF)
                dve.wait_ge(xs_hid, hf + 1)
                dve.tensor_tensor(xs_l[:, cols], xs_f[:], f(xs_h[:, cols]), ALU.subtract)\
                   .then_inc(xs_lod, 1)
                if hf == 0:
                    stack_lo(bu_s, bu_raw, bs_hi, 2, bu_lod)
                dve.wait_ge(u_hid, hf + 1)
                dve.scalar_tensor_tensor(out=u_s[32:64, cols], in0=ps[32:64, 3 + hf, :], scalar=LORA_SCALE,
                                         in1=f(u_s[32:64, cols]), op0=ALU.mult, op1=ALU.subtract)\
                   .then_inc(u_lod, 1)

            def split_p(m, turn):
                dve.wait_ge(pT_hid, at(m + 1, BODY, turn))
                dve.tensor_tensor(pT_l[:], ps[:, 4, :], f(pT_h[:]), ALU.subtract).then_inc(pT_lod, 1)

            def split_c(b):
                cols = slice((b % 4) * S, (b % 4 + 1) * S)
                dve.wait_ge(t3_hi, b + 1)
                dve.tensor_tensor(xc_l[:, :, cols], ps[:, t3_bank[b], :].rearrange("p (k t) -> p k t", k=KC),
                                  f(xc_h[:, :, cols]), ALU.subtract).then_inc(t3_lo, 1)
                if b == 4:
                    dve.wait_ge(xs_lod, 1)
                dve.tensor_reduce(xs_f[:, cols], ps[:, t3_bank[b], :].rearrange("p (k t) -> p t k", k=KC),
                                  AX.X, ALU.add).then_inc(xsum, 1)

            def norm_c(b):
                dve.wait_ge(powd, B // 2 + B + 1 + b)
                if b >= 2:
                    dve.wait_ge(t3, b - 1)
                elif b == 0:
                    dve.wait_ge(tile_mm, TE * 2 * KV)
                apply_norm(xn3[:, b % 2, :], 2, b).then_inc(xnd, 1)

            def split_o(m):
                dve.tensor_tensor(o_l[:], ps[:, 5, :], f(o_h[:]), ALU.subtract).then_inc(o_lod, 1)

            def slot(n, turn=None):
                b = n % B
                if n >= TAIL + 1:
                    dve.wait_ge(o_hid, n - 1)
                    split_o(n - 2)
                if n < SLOTS:
                    if n >= 2:
                        dve.wait_ge(pT, at(n - 1, BODY, turn))
                    dve.wait_ge(scored, at(n + 1, BODY, turn))
                    dve.tensor_tensor(pr[:, n % 2], scores[:, :, 1, :],
                                      maskq[:, b:b + 1, :].to_broadcast([P, HG, S]), ALU.add)\
                       .then_inc(mask_added, 1)
                if 2 <= n < TAIL + 1:
                    dve.wait_ge(o_hid, at(n - 1, BODY, turn))
                if n < SLOTS:
                    dve.wait_ge(mask_added, at(n + 1, BODY, turn))
                if 2 <= n < TAIL + 1:
                    split_o(n - 2)
                if n < SLOTS:
                    for h in range(HG):
                        last = dve.tensor_tensor_reduce(pr[:, n % 2, h, :], scores[:, h, 0, :],
                                                        pr[:, n % 2, h, :], 1.0, LOWEST, ALU.add, ALU.max,
                                                        mx[:, n % 2, h:h + 1])
                    last.then_inc(masked, 1)
                    dve.wait_ge(masked, at(n + 1, BODY, turn))
                    dve.tensor_scalar(nmx[:, n % 2, :], mx[:, n % 2, :], -1.0, None, ALU.mult)\
                       .then_inc(maxed, 1)
                if n == SLOTS + 1:
                    split_sum(0)
                for t in tiles_of(n)[:-1]:
                    rope(t, turn)
                if 1 <= n <= SLOTS:
                    split_p(n - 1, turn)
                if n >= TAIL + 2:
                    norm_c(n - TAIL - 2)
                if n >= TAIL + 1:
                    dve.wait_ge(accd, n - 2)
                    norm_stats(2, n - TAIL - 1)
                if n < SLOTS:
                    dve.wait_ge(expd, at(n + 1, BODY, turn))
                    if n >= 2:
                        dve.wait_ge(normd, at(n - 1, BODY, turn))
                    dve.reciprocal(rc[:, n % 2, :], rs[:, n % 2, :]).then_inc(recd, 1)
                if n >= TAIL + 3:
                    split_c(n - TAIL - 3)
                for t in tiles_of(n)[-1:]:
                    rope(t, turn)
                if n >= 2:
                    m = n - 2
                    dve.wait_ge(womm, at(m + 1, BODY, turn))
                    if m >= B:
                        dve.wait_ge(accd, at(m - B + 1, BODY, turn))
                    dve.tensor_tensor(xres[:, m % B, :], ps[:, 6, :], xres[:, m % B, :], ALU.add)\
                       .then_inc(accd, 1)
                if n == SLOTS + 1:
                    dve.wait_ge(accd, SLOTS)
                    norm_stats(2, B - 1)
                if makes_values(n):
                    dve.wait_ge(v_hid, at(value_count(n), VPT, turn))
                    for i in range(2):
                        hi, lo = values_of(n + B * i)
                        last = dve.tensor_tensor(lo, ps[:, 7, i * P:(i + 1) * P], f(hi), ALU.subtract)
                    last.then_inc(v_lod, 1)

            def gated_tile(i):
                hf, t, j, rows = up_of(i)
                return gsum[0:rows, t, :] if j == 0 else gate[0:rows, i % 2, :]

            def gate_up(i):
                hf, t, j, rows = up_of(i)
                dve.wait_ge(sild, i + 1)
                if j == 0 and hf == 1:
                    dve.wait_ge(gs_lod, t + 1)
                if i >= 3:
                    dve.wait_ge(l_dve, weighed(i - 2))
                if j and i >= 3:
                    dve.wait_ge(gsd, 3 * (i // 4) + max(j - 2, 0))
                    if j % 2:
                        dve.wait_ge(prodd, i // 2)
                dve.tensor_tensor(gated_tile(i), ps[0:rows, 2 + i % 2, :], sil[0:rows, i % 2, :], ALU.mult)\
                   .then_inc(gated, 1)

            def weigh(i):
                hf, t, j, rows = up_of(i)
                dve.wait_ge(gated, i + 1)
                for r in range(RANK):
                    if r == 1 and i % 2 and i < 2 * UPS - 1:
                        continue
                    c = a2c[0:rows, t * 4 + j, r:r + 1]
                    if i % UPS == 0:
                        dve.tensor_scalar(lacc[hf][:, r, :], gated_tile(i), c, None, ALU.mult)\
                           .then_inc(l_dve, 1)
                    else:
                        dve.wait_ge(l_dve, weighed(i - 2 if r and i % 2 == 0 else i - 1)
                                    - (r == 0 and i % 2))
                        dve.scalar_tensor_tensor(out=lacc[hf][0:rows, r, :], in0=gated_tile(i), scalar=c,
                                                 in1=lacc[hf][0:rows, r, :], op0=ALU.mult, op1=ALU.add)\
                           .then_inc(l_dve, 1)

            def split_gs(hf, t):
                rows = min(P, FQ - t * P)
                dve.wait_ge(gs_hid, hf * FT + t + 1)
                dve.tensor_tensor(gs_l[0:rows, t, :], gsum[0:rows, t, :], f(gs_h[0:rows, t, :]),
                                  ALU.subtract).then_inc(gs_lod, 1)

            def sum_lora(hf):
                dve.wait_ge(l_dve, (hf + 1) * UPS * 3 // 2 + hf)
                dve.wait_ge(l_pool, (hf + 1) * (UPS // 2 - 1) - hf)
                dve.tensor_tensor(lacc[hf][:, 1, :], lacc[hf][:, 1, :], lacc[hf][:, RANK, :], ALU.add)\
                   .then_inc(l_sum, 1)

            def split_lora(hf):
                dve.wait_ge(l_hid, hf + 1)
                dve.tensor_tensor(lo_l[:], lacc[hf][:, 0:RANK, :], f(lo_h[:]), ALU.subtract)\
                   .then_inc(l_lod, 1)

            def split_v(hf):
                dve.wait_ge(v3_hi, hf + 1)
                dve.scalar_tensor_tensor(out=v_s[32:64, :], in0=ps[32:64, 6, :], scalar=LORA_SCALE,
                                         in1=f(v_s[32:64, :]), op0=ALU.mult, op1=ALU.subtract)\
                   .then_inc(v3_lo, 1)

            def add_out(b):
                dve.wait_ge(down, b + 1)
                if b >= 4:
                    dve.wait_ge(stored[b % 4], 16)
                dve.tensor_tensor(ost[:, b % 4, :], ps[:, down_bank[b], :], xres[:, b, :], ALU.add)\
                   .then_inc(outd, 1)

            dve.wait_ge(in_mask, 16)
            for n in range(FIRST):
                slot(n)
            with dve.Fori(0, TURNS) as turn:
                for n in loop_slots:
                    slot(n, turn)
            for n in tail_slots:
                slot(n)
                if n == SLOTS + 1:
                    stack_lo(bd_s, bd_raw, bd_hi, 1, bd_lo)
            dve.wait_ge(in_ff[3], 16)
            for i in range(2 * UPS):
                gate_up(i)
                if i:
                    weigh(i - 1)
                if i == UPS + 5:
                    for b in range(4):
                        add_out(b)
                if i % 4 == 1 and i > 1:
                    split_gs((i // 4 - 1) // FT, (i // 4 - 1) % FT)
                if i < 2:
                    norm_c(B - 2 + i)
                if i == 1:
                    split_c(5)
                if i == 3:
                    split_c(6)
                if i == 5:
                    split_c(7)
                if i == 7:
                    split_sum(1)
                if i == UPS + 1:
                    sum_lora(0)
                if i == UPS + 2:
                    split_lora(0)
                if i == UPS + 4:
                    split_v(0)
            weigh(2 * UPS - 1)
            sum_lora(1)
            split_gs(1, FT - 1)
            split_lora(1)
            split_v(1)
            for b in range(4, B):
                add_out(b)

        @block.gpsimd
        def _(pool):
            def chunk(c, turn=None):
                pool.wait_ge(chunk_hi, at(c + 1, CPT, turn))
                hi, lo = chunk_dst(c)
                pool.tensor_tensor(lo, chunk_src(c), f(hi), ALU.subtract).then_inc(chunk_lo, 1)

            pool.wait_ge(in_cst, 16)

            def inverse_a(i):
                pool.wait_ge(vepd, 2 * i + 2)
                pool.tensor_tensor(rstd[:, 0, 2 * i:2 * i + 2], vep[:, 0, 2 * i:2 * i + 2],
                                   minus_half[:, 0:2], ALU.pow).then_inc(powd, 1)

            def add_rope(t, turn):
                half, e = t // TE, t % TE
                pool.wait_ge(rope_mul, at(t + 1, TPT, turn))
                pool.tensor_tensor(qr[:, half % 2, e, :], qr[:, half % 2, e, :], rot[:, t % 2, :], ALU.add)\
                    .then_inc(rope_add, 1)

            def split_q(n, turn):
                pool.wait_ge(q_hi, at(n + 1, BODY, turn))
                pool.tensor_tensor(qs[:, :, 1, :], qr[:, (n // 4) % 2, :, (n % 4) * P:(n % 4 + 1) * P],
                                   f(qs[:, :, 0, :]), ALU.subtract).then_inc(q_lo, 1)

            inverse_a(0)
            inverse_a(1)
            for c in range(CH_A, CH_A + PRE):
                chunk(c)
            for b in range(B + LAG):
                if b < 2:
                    inverse_a(2 + b)
                if b < B:
                    pool.wait_ge(gel, b + 1)
                    pool.tensor_tensor(xres[:, b, :], xres[:, b, :], yb[:, b % 2, :], ALU.add)\
                        .then_inc(x1d, 1)
                if 1 <= b <= B:
                    pool.wait_ge(vepd, B + b)
                    pool.tensor_tensor(rstd[:, 1, b - 1:b], vep[:, 1, b - 1:b], minus_half[:, 0:1], ALU.pow)\
                        .then_inc(powd, 1)
                for c in early_chunks(b):
                    chunk(c)
                for t in early_tiles.get(b, []):
                    add_rope(t, None)
                    if t == TE - 1:
                        split_q(0, None)

            def slot(n, turn=None):
                if n + 1 < SLOTS:
                    split_q(n + 1, turn)
                if n < SLOTS:
                    pool.wait_ge(recd, at(n + 1, BODY, turn))
                    pool.tensor_tensor(pr[:, n % 2], pr[:, n % 2],
                                       rc[:, n % 2, :].rearrange("p (h a) -> p h a", a=1)
                                       .to_broadcast([P, HG, P]), ALU.mult).then_inc(normd, 1)
                for c in chunks_of(n):
                    chunk(c, turn)
                for t in tiles_of(n):
                    add_rope(t, turn)

            for n in range(FIRST):
                slot(n)
            with pool.Fori(0, TURNS) as turn:
                for n in loop_slots:
                    slot(n, turn)
            def inverse_c(b):
                pool.wait_ge(vepd, 2 * B + b + 1)
                pool.tensor_tensor(rstd[:, 2, b:b + 1], vep[:, 2, b:b + 1], minus_half[:, 0:1], ALU.pow)\
                    .then_inc(powd, 1)

            for n in tail_slots:
                slot(n)
                if n == TAIL + 2:
                    pool.wait_ge(a_hi, 1)
                    pool.tensor_tensor(a_l[:], a_raw[:], f(a_h[:]), ALU.subtract).then_inc(a_lo, 1)
                if TAIL + 3 <= n <= SLOTS:
                    i, piece = divmod(n - TAIL - 3, 2)
                    hi, lo, raw = ((g1_h, g1_l, g1_raw), (g3_h, g3_l, g3_raw))[i]
                    cols = slice(piece * FF // 2, (piece + 1) * FF // 2)
                    pool.wait_ge(g_hi, i + 1)
                    pool.tensor_tensor(lo[:, cols], raw[:, cols], f(hi[:, cols]), ALU.subtract)\
                        .then_inc(g_lo, 1)
                if n >= TAIL + 1:
                    inverse_c(n - TAIL - 1)
                if n == SLOTS:
                    pool.wait_ge(powd, B // 2 + 2 * B - 2)
                    pool.wait_ge(bs_hi, 1)
                    pool.tensor_tensor(bg_s[64:STK, :], bg_raw[64:STK, :], f(bg_s[64:STK, :]), ALU.subtract)\
                        .then_inc(bg_lod, 1)
                    pool.wait_ge(bg_lod, 1)
            inverse_c(B - 1)
            pool.wait_ge(womm, SLOTS)
            pool.wait_ge(g2_hi, 1)
            pool.tensor_tensor(g2_l[:, 0:FT - 1, :], g2_raw[:, 0:FT - 1, :],
                               f(g2_h[:, 0:FT - 1, :]), ALU.subtract)
            r = FQ - (FT - 1) * P
            pool.tensor_tensor(g2_l[0:r, FT - 1, :], g2_raw[0:r, FT - 1, :],
                               f(g2_h[0:r, FT - 1, :]), ALU.subtract).then_inc(g2_lo, 1)
            for i in range(2 * UPS):
                hf, t, j, rows = up_of(i)
                if j == 1:
                    pool.wait_ge(l_dve, weighed(i - 1))
                if j:
                    pool.wait_ge(gated, i + 1)
                    if i > 1:
                        pool.wait_ge(gsd, 3 * (i // 4) + j - 1)
                    pool.tensor_tensor(gsum[0:rows, t, :], gsum[0:rows, t, :], gate[0:rows, i % 2, :],
                                       ALU.add).then_inc(gsd, 1)
                if i % 2 and i % UPS != 1 and i < 2 * UPS - 1:
                    pool.wait_ge(prodd, (i + 1) // 2)
                    if i > 3:
                        pool.wait_ge(l_pool, i // 2 - 1 - hf)
                    pool.tensor_tensor(lacc[hf][0:rows, RANK, :], lacc[hf][0:rows, RANK, :], prod[0:rows, :],
                                       ALU.add).then_inc(l_pool, 1)


def _rope_tables():
    inv = 1.0 / 10000.0 ** (np.arange(0, DK, 2, dtype=np.float32) / np.float32(DK))
    ang = np.arange(S, dtype=np.float32)[None, :] * inv.astype(np.float32)[:, None]
    share = np.float64(DK) ** -0.25
    c, s = np.cos(ang.astype(np.float32)) * share, np.sin(ang.astype(np.float32)) * share
    return np.concatenate([c, c]).astype(np.float32), np.concatenate([s, -s]).astype(np.float32)


def _stack(rows, at_row):
    st = np.zeros((STK, rows.shape[1]), rows.dtype)
    for g in range(3):
        st[32 * g + at_row:32 * g + at_row + RANK] = rows
    return st


def kernel(x, ctx_4096, mask_BxSxS2_ff0, L0_attn_w1, L0_attn_w2, L0_attn_b2, L0_attn_sparse_mask,
           L0_xattn_wq, L0_xattn_wk, L0_xattn_wv, L0_xattn_wo, L0_ffn_w1q, L0_ffn_a1, L0_ffn_b1,
           L0_ffn_w3q, L0_ffn_a3, L0_ffn_b3, L0_ffn_w2q, L0_ffn_a2, L0_ffn_b2):
    import concourse.bacc as _bacc
    from concourse.bass_utils import run_bass_kernel_spmd as _run

    a = np.asarray
    f32 = a(x).dtype
    stream = np.empty((NCH, P, 512), f32)
    w1, w2t = a(L0_attn_w1), a(L0_attn_w2).T
    ctxT = a(ctx_4096).reshape(TOK, D).T
    for k in range(KC):
        stream[2 * k] = w1[k * P:(k + 1) * P]
        stream[2 * k + 1] = w2t[k * P:(k + 1) * P]
        for hf in range(2):
            stream[CH_A + 2 * k + hf] = ctxT[k * P:(k + 1) * P, hf * HALF:(hf + 1) * HALF]

    def heads(w):
        w = a(w)
        return w.reshape(KC, P, -1, P).transpose(2, 1, 0, 3).reshape(-1, P, KC * P)
    weights = {"k": heads(L0_xattn_wk), "q": heads(L0_xattn_wq), "v": heads(L0_xattn_wv),
               "o": a(L0_xattn_wo).reshape(QH, P, D)}
    for c in range(CH0, NCH):
        g, (kind, i) = place_of(c)
        stream[c] = weights[kind][{"k": g, "v": g + i}.get(kind, HG * g + i)]

    cosT, sinT = _rope_tables()
    sel = np.zeros((P, RANK, STK), np.float32)
    for r in range(RANK):
        sel[:, r, r::32] = 1.0
    ones = np.zeros((P, P), np.float32)
    ones[0:64:32] = 1.0
    consts = np.concatenate([np.eye(P, dtype=np.float32), cosT, sinT, ones, sel.reshape(P, -1),
                             np.full((P, B), -0.5, np.float32)], axis=1)
    b2 = np.zeros((64, D), f32)
    b2[0::32] = a(L0_attn_b2)
    a_cols = np.ascontiguousarray((_stack(a(L0_ffn_a1), 0)[:, :]).T)
    a3 = _stack(a(L0_ffn_a3), RANK).T
    for g in range(3):
        a_cols[:, 32 * g + RANK:32 * g + 2 * RANK] = a3[:, 32 * g + RANK:32 * g + 2 * RANK]
    a2 = a(L0_ffn_a2).reshape(RANK, 4, FQ)
    a2_cols = np.zeros((P, FT, 4, RANK), f32)
    for t in range(FT):
        rows = min(P, FQ - t * P)
        a2_cols[:rows, t] = a2[:, :, t * P:t * P + rows].transpose(2, 1, 0)
    arrays = {
        "stream": stream, "x": a(x), "mask": a(mask_BxSxS2_ff0), "consts": consts,
        "spmask": a(L0_attn_sparse_mask), "b2": b2,
        "w1q": a(L0_ffn_w1q).T, "w3q": a(L0_ffn_w3q).T, "w2q": a(L0_ffn_w2q).T,
        "a_cols": a_cols, "bg_rows": _stack(a(L0_ffn_b1).T, 0), "bu_rows": _stack(a(L0_ffn_b3).T, RANK),
        "a2_cols": a2_cols.reshape(P, FT * 4, RANK), "b2_rows": _stack(a(L0_ffn_b2).T, 0),
    }
    nc = _bacc.Bacc("TRN2", target_bir_lowering=False, num_devices=1)
    given, args = {}, []
    for name, v in arrays.items():
        v = np.ascontiguousarray(v)
        given[f"in_{name}"] = v
        args.append(nc.dram_tensor(f"in_{name}", v.shape, mybir.dt.from_np(v.dtype), kind="ExternalInput").ap())
    args.append(nc.dram_tensor("out", (B, S, D), F32, kind="ExternalOutput").ap())
    decoder_block(nc, *args)
    r = _run(nc, [given], core_ids=[0])
    return r.results[0]["out"]
```
